# Optimizing a Trainium2 kernel written in Bass

```python
import numpy as np
import jax
import jax.numpy as jnp

def _softmax(x, axis=-1):
    return jax.nn.softmax(x, axis=axis)

def _gelu(x):
    return jax.nn.gelu(x, approximate=True)

def _silu(x):
    return jax.nn.silu(x)

def _sigmoid(x):
    return jax.nn.sigmoid(x)

def _layernorm(x, axis=-1, eps=1e-05):
    m = jnp.mean(x, axis=axis, keepdims=True)
    v = jnp.var(x, axis=axis, keepdims=True)
    return (x - m) / jnp.sqrt(v + eps)

def _scatter_add(tgt, idx, src, axis=0):
    return tgt.at[idx].add(src)

def _segment_sum(src, seg, n):
    return jax.ops.segment_sum(src, seg, n)
kernel_name = 'mk_adj_preln_d1_adj_r2_5e1ae0'

def setup_inputs(seed: int=0):
    np.random.seed(seed)
    _w = jnp.asarray

    def _rec_inputs():
        import jax
        import jax.numpy as jnp
        _gk = jax.random.key(seed)
        x = 1.444e-06 + 0.02 * jax.random.normal(jax.random.fold_in(_gk, 1), (32, 256, 512), jnp.float32)
        _a = jax.random.bernoulli(jax.random.fold_in(_gk, 2), 0.03125, (32, 256, 256))
        _a = jnp.logical_or(_a, jnp.eye(256, dtype=bool))
        _af = _a.astype(jnp.float32)
        adj = _af
        return (x, adj)
    x, adj = _rec_inputs()

    def _L0_gnn_setup():
        import jax, jax.numpy as jnp
        import numpy as np
        B, N, D, H = (4, 1024, 512, 8)
        HD = D // H
        SCALE = HD ** (-0.5)
        LN_EPS = 1e-05

        def _lin(x, w, b):
            return x @ w.T + b

        def _ln(x, g, b):
            m = x.mean(-1, keepdims=True)
            v = ((x - m) ** 2).mean(-1, keepdims=True)
            return (x - m) / jnp.sqrt(v + LN_EPS) * g + b

        def _attn(q, k, v, mask):
            Bq, Nt, _ = q.shape
            Ns = k.shape[1]
            qh = q.reshape(Bq, Nt, H, HD).transpose(0, 2, 1, 3)
            kh = k.reshape(Bq, Ns, H, HD).transpose(0, 2, 1, 3)
            vh = v.reshape(Bq, Ns, H, HD).transpose(0, 2, 1, 3)
            scores = jnp.einsum('bhid,bhjd->bhij', qh, kh) * SCALE
            scores = jnp.where(mask[:, None] > 0, scores, -jnp.inf)
            w = jax.nn.softmax(scores, axis=-1)
            out = jnp.einsum('bhij,bhjd->bhid', w, vh)
            return out.transpose(0, 2, 1, 3).reshape(Bq, Nt, D)
        key = jax.random.key(seed)
        ks = jax.random.split(key, 16)
        pe = jax.random.normal(ks[0], (B, N, D), jnp.float32) * 0.02
        inc = jax.random.randint(ks[1], (B, N, N), 0, 2).astype(jnp.float32)
        inc = jnp.maximum(inc, jnp.eye(N, dtype=jnp.float32)[None])

        def w(k, o, i):
            return jax.random.normal(k, (o, i), jnp.float32) / np.sqrt(i)
        inp = {'prompt_embeddings': pe, 'incidence_matrix': inc, 'n2e_q_w': w(ks[2], D, D), 'n2e_q_b': jnp.zeros((D,), jnp.float32), 'n2e_k_w': w(ks[3], D, D), 'n2e_k_b': jnp.zeros((D,), jnp.float32), 'n2e_v_w': w(ks[4], D, D), 'n2e_v_b': jnp.zeros((D,), jnp.float32), 'e2n_q_w': w(ks[5], D, D), 'e2n_q_b': jnp.zeros((D,), jnp.float32), 'e2n_k_w': w(ks[6], D, D), 'e2n_k_b': jnp.zeros((D,), jnp.float32), 'e2n_v_w': w(ks[7], D, D), 'e2n_v_b': jnp.zeros((D,), jnp.float32), 'norm1_g': jnp.ones((D,), jnp.float32), 'norm1_b': jnp.zeros((D,), jnp.float32), 'norm2_g': jnp.ones((D,), jnp.float32), 'norm2_b': jnp.zeros((D,), jnp.float32), 'norm3_g': jnp.ones((D,), jnp.float32), 'norm3_b': jnp.zeros((D,), jnp.float32), 'ffn_w1': w(ks[8], 4 * D, D), 'ffn_b1': jnp.zeros((4 * D,), jnp.float32), 'ffn_w2': w(ks[9], D, 4 * D), 'ffn_b2': jnp.zeros((D,), jnp.float32)}
        return inp
    _L0_gnn_all = _L0_gnn_setup()
    _L0_gnn_in = {k: v for k, v in _L0_gnn_all.items() if k in ('n2e_q_w', 'n2e_q_b', 'n2e_k_w', 'n2e_k_b', 'n2e_v_w', 'n2e_v_b', 'e2n_q_w', 'e2n_q_b', 'e2n_k_w', 'e2n_k_b', 'e2n_v_w', 'e2n_v_b', 'norm1_g', 'norm1_b', 'norm2_g', 'norm2_b', 'norm3_g', 'norm3_b', 'ffn_w1', 'ffn_b1', 'ffn_w2', 'ffn_b2')}
    del _L0_gnn_all
    return {'x': x, 'adj': adj, 'L0_gnn_n2e_q_w': _L0_gnn_in['n2e_q_w'], 'L0_gnn_n2e_q_b': _L0_gnn_in['n2e_q_b'], 'L0_gnn_n2e_k_w': _L0_gnn_in['n2e_k_w'], 'L0_gnn_n2e_k_b': _L0_gnn_in['n2e_k_b'], 'L0_gnn_n2e_v_w': _L0_gnn_in['n2e_v_w'], 'L0_gnn_n2e_v_b': _L0_gnn_in['n2e_v_b'], 'L0_gnn_e2n_q_w': _L0_gnn_in['e2n_q_w'], 'L0_gnn_e2n_q_b': _L0_gnn_in['e2n_q_b'], 'L0_gnn_e2n_k_w': _L0_gnn_in['e2n_k_w'], 'L0_gnn_e2n_k_b': _L0_gnn_in['e2n_k_b'], 'L0_gnn_e2n_v_w': _L0_gnn_in['e2n_v_w'], 'L0_gnn_e2n_v_b': _L0_gnn_in['e2n_v_b'], 'L0_gnn_norm1_g': _L0_gnn_in['norm1_g'], 'L0_gnn_norm1_b': _L0_gnn_in['norm1_b'], 'L0_gnn_norm2_g': _L0_gnn_in['norm2_g'], 'L0_gnn_norm2_b': _L0_gnn_in['norm2_b'], 'L0_gnn_norm3_g': _L0_gnn_in['norm3_g'], 'L0_gnn_norm3_b': _L0_gnn_in['norm3_b'], 'L0_gnn_ffn_w1': _L0_gnn_in['ffn_w1'], 'L0_gnn_ffn_b1': _L0_gnn_in['ffn_b1'], 'L0_gnn_ffn_w2': _L0_gnn_in['ffn_w2'], 'L0_gnn_ffn_b2': _L0_gnn_in['ffn_b2']}

def reference(x, adj, L0_gnn_n2e_q_w, L0_gnn_n2e_q_b, L0_gnn_n2e_k_w, L0_gnn_n2e_k_b, L0_gnn_n2e_v_w, L0_gnn_n2e_v_b, L0_gnn_e2n_q_w, L0_gnn_e2n_q_b, L0_gnn_e2n_k_w, L0_gnn_e2n_k_b, L0_gnn_e2n_v_w, L0_gnn_e2n_v_b, L0_gnn_norm1_g, L0_gnn_norm1_b, L0_gnn_norm2_g, L0_gnn_norm2_b, L0_gnn_norm3_g, L0_gnn_norm3_b, L0_gnn_ffn_w1, L0_gnn_ffn_b1, L0_gnn_ffn_w2, L0_gnn_ffn_b2):
    import jax
    import jax.numpy as jnp

    def _L0_gnn_ref(prompt_embeddings, incidence_matrix, n2e_q_w, n2e_q_b, n2e_k_w, n2e_k_b, n2e_v_w, n2e_v_b, e2n_q_w, e2n_q_b, e2n_k_w, e2n_k_b, e2n_v_w, e2n_v_b, norm1_g, norm1_b, norm2_g, norm2_b, norm3_g, norm3_b, ffn_w1, ffn_b1, ffn_w2, ffn_b2):
        import jax, jax.numpy as jnp
        import numpy as np
        B, N, D, H = (4, 1024, 512, 8)
        HD = D // H
        SCALE = HD ** (-0.5)
        LN_EPS = 1e-05

        def _lin(x, w, b):
            return x @ w.T + b

        def _ln(x, g, b):
            m = x.mean(-1, keepdims=True)
            v = ((x - m) ** 2).mean(-1, keepdims=True)
            return (x - m) / jnp.sqrt(v + LN_EPS) * g + b

        def _attn(q, k, v, mask):
            Bq, Nt, _ = q.shape
            Ns = k.shape[1]
            qh = q.reshape(Bq, Nt, H, HD).transpose(0, 2, 1, 3)
            kh = k.reshape(Bq, Ns, H, HD).transpose(0, 2, 1, 3)
            vh = v.reshape(Bq, Ns, H, HD).transpose(0, 2, 1, 3)
            scores = jnp.einsum('bhid,bhjd->bhij', qh, kh) * SCALE
            scores = jnp.where(mask[:, None] > 0, scores, -jnp.inf)
            w = jax.nn.softmax(scores, axis=-1)
            out = jnp.einsum('bhij,bhjd->bhid', w, vh)
            return out.transpose(0, 2, 1, 3).reshape(Bq, Nt, D)
        pe = prompt_embeddings
        n2e_mask = incidence_matrix.transpose(0, 2, 1)
        eq = _lin(pe, n2e_q_w, n2e_q_b)
        nk = _lin(pe, n2e_k_w, n2e_k_b)
        nv = _lin(pe, n2e_v_w, n2e_v_b)
        edge_features = _attn(eq, nk, nv, n2e_mask)
        edge_features = _ln(edge_features + pe, norm1_g, norm1_b)
        nq = _lin(pe, e2n_q_w, e2n_q_b)
        ek = _lin(edge_features, e2n_k_w, e2n_k_b)
        ev = _lin(edge_features, e2n_v_w, e2n_v_b)
        node_updates = _attn(nq, ek, ev, incidence_matrix)
        node_features = _ln(pe + node_updates, norm2_g, norm2_b)
        h = jax.nn.gelu(_lin(node_features, ffn_w1, ffn_b1), approximate=False)
        out = _ln(node_features + _lin(h, ffn_w2, ffn_b2), norm3_g, norm3_b)
        return out
    h = jnp.maximum(_layernorm(x, axis=-1), 0.0)
    x = x + _L0_gnn_ref(h, adj, L0_gnn_n2e_q_w, L0_gnn_n2e_q_b, L0_gnn_n2e_k_w, L0_gnn_n2e_k_b, L0_gnn_n2e_v_w, L0_gnn_n2e_v_b, L0_gnn_e2n_q_w, L0_gnn_e2n_q_b, L0_gnn_e2n_k_w, L0_gnn_e2n_k_b, L0_gnn_e2n_v_w, L0_gnn_e2n_v_b, L0_gnn_norm1_g, L0_gnn_norm1_b, L0_gnn_norm2_g, L0_gnn_norm2_b, L0_gnn_norm3_g, L0_gnn_norm3_b, L0_gnn_ffn_w1, L0_gnn_ffn_b1, L0_gnn_ffn_w2, L0_gnn_ffn_b2)
    return x

_drawn_inputs = setup_inputs


def setup_inputs(seed=0):
    import zlib

    import numpy as np

    out = dict(_drawn_inputs(seed))
    spreads = {'L0_gnn_n2e_q_b': (0.0, 0.8),
     'L0_gnn_n2e_k_b': (0.0, 0.8),
     'L0_gnn_n2e_v_b': (0.0, 0.1),
     'L0_gnn_e2n_q_b': (0.0, 0.282),
     'L0_gnn_e2n_k_b': (0.0, 0.8),
     'L0_gnn_e2n_v_b': (0.0, 0.1),
     'L0_gnn_norm1_g': (1.0, 0.2),
     'L0_gnn_norm1_b': (0.0, 0.1),
     'L0_gnn_norm2_g': (1.0, 0.2),
     'L0_gnn_norm2_b': (0.0, 0.1),
     'L0_gnn_norm3_g': (1.0, 0.2),
     'L0_gnn_norm3_b': (0.0, 0.1),
     'L0_gnn_ffn_b1': (0.0, 0.1),
     'L0_gnn_ffn_b2': (0.0, 0.1)}
    factors = {}
    for name, (base, spread) in spreads.items():
        noise = np.random.default_rng([zlib.crc32(name.encode()), seed]).standard_normal(out[name].shape)
        drawn = base * np.exp(spread * noise) if base else spread * noise
        out[name] = jnp.asarray(drawn.astype(out[name].dtype))
    for name, factor in factors.items():
        out[name] = (out[name] * factor).astype(out[name].dtype)
    return out
```

```python
from contextlib import ExitStack

import concourse.bass as bass
from concourse import mybir

F32 = mybir.dt.float32
F32R = mybir.dt.float32r
BF16 = mybir.dt.bfloat16
ALU = mybir.AluOpType
ACT = mybir.ActivationFunctionType
AX_X = mybir.AxisListType.X

P = 128
B, N, D, H = 32, 256, 512, 8
HD = D // H
FF = 4 * D
DC = D // P
NT = N // P
PAIRS = H // 2
FT = FF // P
ROWS = 4 * P
RT = ROWS // P
PASSES = B * N // ROWS
SCALE = HD ** -0.5
LN_EPS = 1e-5
MASKED = -1e30
GROUPS = 8
BN_S, BN_A = 6, 2

COLUMN_VECTORS = ["n2e_q_b", "n2e_k_b", "e2n_q_b", "e2n_k_b", "norm1_g", "norm1_b"]
WEIGHTS = ["n2e_q_w", "n2e_k_w", "n2e_v_w", "e2n_q_w", "e2n_k_w", "e2n_v_w"]


def hold(engine, passed):
    engine.sem_inc(passed, 1)


class Half:

    def __init__(self, att, batch, par, pos, before=None, side=None, ahead=True):
        self.att, self.batch, self.par, self.pos = att, batch, par, pos
        self.before, self.side, self.ahead = before, side, ahead
        self.head0 = pos * H


class Side:

    def __init__(self, att, batch, par):
        self.att, self.batch, self.par = att, batch, par
        if att == 1:
            self.first = 0 if isinstance(batch, int) and batch == 0 else 2 * GROUPS * batch - GROUPS
        elif isinstance(batch, int) and batch == B - 1:
            self.first = (2 * B - 1) * GROUPS
        else:
            self.first = 2 * GROUPS * batch + 2 * GROUPS


def first_half(k, par, before=True, side=True, ahead=True):
    return Half(1, k, par, 2 * k - 1,
                before=Half(2, k - 2, par, 2 * k - 2) if before else None,
                side=Side(2, k - 1, 1 - par) if side else None, ahead=ahead)


def second_half(k, par, side=True, ahead=True):
    return Half(2, k, par, 2 * k + 2,
                before=Half(1, k + 1, 1 - par, 2 * k + 1),
                side=Side(1, k + 2, par) if side else None, ahead=ahead)


def at_least(engine, semaphore, value):
    if isinstance(value, int) and value <= 0:
        return
    engine.wait_ge(semaphore, value)


def attention_part(nc, x, adj, adj_t, w, columns, bv1_row, bv2_row, peeled_rows, node_rows):
    with ExitStack() as ctx:
        def sb(name, shape, dt=F32):
            return ctx.enter_context(nc.sbuf_tensor(name, shape, dt))

        def ps(name):
            return ctx.enter_context(nc.psum_tensor(name, [P, 512], F32))

        def sem(name):
            return ctx.enter_context(nc.semaphore(name))

        w_hi = {n: sb(f"{n}_hi", [P, DC, D], F32R) for n in WEIGHTS}
        w_lo = {n: sb(f"{n}_lo", [P, DC, D], F32R) for n in WEIGHTS}
        q_hi = {a: sb(f"q{a}_hi", [P, H, N], F32R) for a in (1, 2)}
        q_lo = {a: sb(f"q{a}_lo", [P, H, N], F32R) for a in (1, 2)}
        k_hi = {a: sb(f"k{a}_hi", [P, DC, N], F32R) for a in (1, 2)}
        k_lo = {a: sb(f"k{a}_lo", [P, DC, N], F32R) for a in (1, 2)}
        v_both = {a: sb(f"v{a}", [P, NT, H, P], F32R) for a in (1, 2)}
        pe_t_hi = [sb(f"pe_t_hi{i}", [P, DC, N], F32R) for i in range(2)]
        pe_t_lo = [sb(f"pe_t_lo{i}", [P, DC, N], F32R) for i in range(2)]
        edge_t_hi = sb("edge_t_hi", [P, DC, N], F32R)
        edge_t_lo = sb("edge_t_lo", [P, DC, N], F32R)
        pe = [sb(f"pe{i}", [P, NT, D]) for i in range(2)]
        pe_again = sb("pe_again", [P, NT, D])
        adj_raw = sb("adj_raw", [P, NT, N])
        mask = {a: sb(f"mask{a}", [P, NT, N], BF16) for a in (1, 2)}
        probs = sb("probs", [P, NT, N])
        probs_t_hi = sb("probs_t_hi", [P, NT, N], F32R)
        probs_t_lo = sb("probs_t_lo", [P, NT, N], F32R)
        heads_t = sb("heads_t", [P, 2, N])
        rows = {a: sb(f"rows{a}", [P, PAIRS, NT * P]) for a in (1, 2)}
        bv_row = {a: sb(f"bv{a}_row", [P, D]) for a in (1, 2)}
        col = {n: sb(f"{n}_col", [P, DC]) for n in COLUMN_VECTORS}
        ident = sb("ident", [P, P])
        neg_half = sb("neg_half", [P, NT])
        neg_max = sb("neg_max", [P, 2, NT])
        sums = {a: sb(f"sums{a}", [P, NT, H]) for a in (1, 2)}
        inv_sums = sb("inv_sums", [P, NT, H])
        x_stats, row_stats = sb("x_stats", [P, NT, BN_S]), sb("row_stats", [P, NT, BN_S])
        x_mv, row_mv = sb("x_mv", [P, NT, BN_A]), sb("row_mv", [P, NT, BN_A])
        x_var, row_var = sb("x_var", [P, NT]), sb("row_var", [P, NT])
        x_rstd, row_rstd = sb("x_rstd", [P, NT]), sb("row_rstd", [P, NT])
        x_shift = sb("x_shift", [P, NT])
        bias_parts = sb("bias_parts", [P, 2 * DC])

        scores_ps = [ps(f"scores_ps{i}") for i in range(2)]
        probs_t_ps = [ps(f"probs_t_ps{i}") for i in range(2)]
        proj_ps = [ps(f"proj_ps{i}") for i in range(2)]
        heads_ps = ps("heads_ps")
        rows_ps = ps("rows_ps")

        s_vectors = sem("vectors_loaded")
        s_stage = [sem(f"weights_staged{i}") for i in range(2)]
        s_w_hi = sem("weights_hi")
        s_w_lo = sem("weights_lo")
        s_w_scaled = sem("weights_scaled")
        s_w_bias = sem("weight_bias_products")
        s_b_bcast = sem("bias_broadcast")
        s_consts = sem("constants_ready")
        s_zeros = sem("zeros_ready")
        s_biases = sem("biases_ready")
        s_x = sem("x_loaded")
        s_x_stats = sem("x_stats_ready")
        s_x_var = sem("x_var_ready")
        s_x_rstd = sem("x_rstd_ready")
        s_x_shift = sem("x_shift_ready")
        s_pe = sem("pe_ready")
        s_pe_stored = sem("pe_stored")
        s_pe_again = sem("pe_again_loaded")
        s_adj = sem("adj_loaded")
        s_mask = sem("mask_ready")
        s_group = sem("proj_group_done")
        s_hi = sem("proj_hi_ready")
        s_lo = sem("proj_lo_ready")
        s_scores = sem("scores_done")
        s_max = sem("max_ready")
        s_exp = sem("exp_ready")
        s_probs_t = sem("probs_transposed")
        s_pt_hi = sem("probs_t_hi_ready")
        s_pt_lo = sem("probs_t_lo_ready")
        s_pv = sem("values_weighted")
        s_heads_t = sem("heads_t_ready")
        s_rows_ps = sem("rows_transposed")
        s_rows = sem("rows_ready")
        s_inv = sem("inv_sums_ready")
        s_res_step = sem("residual_step")
        s_res = sem("residual_added")
        s_row_stats = sem("row_stats_ready")
        s_row_var = sem("row_var_ready")
        s_row_rstd = sem("row_rstd_ready")
        s_ln = sem("rows_normalised")
        s_node = sem("node_stored")
        s_passed = {e: sem(f"passed_{e}") for e in ("sp", "pool", "dve")}

        HALVES = 2 * len(WEIGHTS)
        CH = DC // 2
        stage = [rows[a][:, :, :].rearrange("p (c a) n -> p c (a n)", c=CH) for a in (1, 2)]

        def mask_number(att, batch):
            if att == 1:
                return 0 if isinstance(batch, int) and batch == 0 else 2 * batch - 1
            if isinstance(batch, int) and batch == B - 1:
                return 2 * B - 1
            return 2 * batch + 2

        def schedule(do_setup, do_project, do_half, do_drain, loop):
            do_setup()
            do_project(Side(1, 0, 0))
            start = Half(1, 0, 0, 0)
            do_half(start)
            do_drain(start)
            do_project(Side(1, 1, 1))
            do_half(first_half(1, 1, before=False))
            with loop(0, (B - 4) // 2) as i:
                for par in (0, 1):
                    do_half(second_half(2 * i + par, par))
                    do_half(first_half(2 * i + par + 2, par))
            do_half(second_half(B - 4, 0))
            do_half(first_half(B - 2, 0))
            do_half(second_half(B - 3, 1, ahead=False))
            do_half(first_half(B - 1, 1, ahead=False))
            end = second_half(B - 2, 0, side=False, ahead=False)
            do_half(end)
            do_drain(end)
            do_project(Side(2, B - 1, 1))
            last = Half(2, B - 1, 1, 2 * B - 1, ahead=False)
            do_half(last)
            do_drain(last)

        block = ctx.enter_context(nc.Block())

        @block.sync
        def _(sp):
            def load_x(batch, par):
                hold(sp, s_passed["sp"])
                sp.dma_start(pe[par][:, :, :], x[bass.ds(batch * N, N), :].rearrange(
                    "(t p) d -> p t d", p=P)).then_inc(s_x, 16)

            def load_adj(att, batch):
                src = adj_t if att == 1 else adj
                hold(sp, s_passed["sp"])
                sp.dma_start(adj_raw[:, :, :], src[bass.ds(batch * N, N), :].rearrange(
                    "(t p) n -> p t n", p=P)).then_inc(s_adj, 16)

            def store_pe(batch, par):
                sp.wait_ge(s_pe, batch + 1)
                hold(sp, s_passed["sp"])
                sp.dma_start(peeled_rows[bass.ds(batch * N, N), :].rearrange(
                    "(t p) d -> p t d", p=P), pe[par][:, :, :]).then_inc(s_pe_stored, 16)

            def store_node(half):
                sp.wait_ge(s_ln, half.pos + 1)
                hold(sp, s_passed["sp"])
                for t in range(NT):
                    sp.dma_start(node_rows[bass.ds(half.batch * N + t * P, P), :].rearrange(
                        "p (c n) -> p c n", c=PAIRS), rows[2][:, :, t * P:(t + 1) * P]).then_inc(s_node, 16)
                sp.wait_ge(s_node, (half.batch + 1) * 16 * NT)
                hold(sp, s_passed["sp"])

            def setup():
                load_x(0, 0)
                load_adj(1, 0)
                for n in COLUMN_VECTORS:
                    sp.dma_start(col[n][:, :], columns[n]).then_inc(s_vectors, 16)
                for a, src in ((1, bv1_row), (2, bv2_row)):
                    sp.dma_start(bv_row[a][:, :], src.to_broadcast([P, D])).then_inc(s_vectors, 16)
                for n in range(HALVES):
                    if n >= 2:
                        sp.wait_ge(s_w_hi, n - 1)
                        hold(sp, s_passed["sp"])
                        sp.wait_ge(s_w_lo, n - 1)
                        hold(sp, s_passed["sp"])
                    src = w[WEIGHTS[n // 2]].rearrange("(c p) o -> p c o", p=P)
                    sp.dma_start(stage[n % 2], src[:, CH * (n % 2):CH * (n % 2) + CH, :]).then_inc(s_stage[n % 2], 16)
                sp.wait_ge(s_x, 16)
                hold(sp, s_passed["sp"])
                load_x(1, 1)

            def project(side):
                pass

            def half(h):
                if h.att == 2:
                    if h.before is not None:
                        sp.wait_ge(s_mask, mask_number(2, h.batch + 1))
                        hold(sp, s_passed["sp"])
                        load_adj(2, h.batch + 1)
                    sp.wait_ge(s_res, 2 * h.batch + 1)
                    hold(sp, s_passed["sp"])
                    sp.wait_ge(s_pe_stored, (h.batch + 1) * 16)
                    hold(sp, s_passed["sp"])
                    sp.dma_start(pe_again[:, :, :], peeled_rows[bass.ds(h.batch * N, N), :].rearrange(
                        "(t p) d -> p t d", p=P)).then_inc(s_pe_again, 16)
                    if h.ahead:
                        sp.wait_ge(s_res, h.before.pos + 1)
                        hold(sp, s_passed["sp"])
                        sp.wait_ge(s_pe_stored, (h.batch + 2) * 16)
                        hold(sp, s_passed["sp"])
                        sp.wait_ge(s_x, (h.batch + 3) * 16)
                        hold(sp, s_passed["sp"])
                        load_x(h.batch + 3, 1 - h.par)
                else:
                    if h.ahead:
                        sp.wait_ge(s_mask, mask_number(1, h.batch + 1))
                        hold(sp, s_passed["sp"])
                        load_adj(1, h.batch + 1)
                        store_pe(h.batch + 1, 1 - h.par)
                    if h.before is not None:
                        store_node(h.before)

            def drain(h):
                if h.att == 2:
                    store_node(h)
                elif h.batch == 0:
                    sp.wait_ge(s_mask, 2)
                    hold(sp, s_passed["sp"])
                    load_adj(2, 0)
                    sp.wait_ge(s_res, 1)
                    hold(sp, s_passed["sp"])
                    sp.wait_ge(s_pe_stored, 32)
                    hold(sp, s_passed["sp"])
                    load_x(2, 0)

            def setup_all():
                setup()
                store_pe(0, 0)

            schedule(setup_all, project, half, drain, sp.Fori)

        @block.gpsimd
        def _(pool):
            def build_mask(att, batch, head0):
                number = mask_number(att, batch)
                pool.wait_ge(s_adj, (number + 1) * 16)
                at_least(pool, s_max, head0)
                hold(pool, s_passed["pool"])
                pool.tensor_scalar(mask[att][:, :, :], adj_raw[:, :, :], 0.0, MASKED, ALU.is_le, ALU.mult)\
                    .then_inc(s_mask, 1)

            def setup():
                pool.memset(ident[:, :], 0.0).then_inc(s_consts, 1)
                pool.wait_ge(s_consts, 1)
                pool.affine_select(out=ident[:, :], in_=ident[:, :], compare_op=ALU.not_equal, fill=1.0,
                                   base=0, pattern=[[-1, P]], channel_multiplier=1).then_inc(s_consts, 1)
                pool.memset(neg_half[:, :], -0.5).then_inc(s_consts, 1)
                pool.wait_ge(s_consts, 3)
                build_mask(1, 0, 0)
                for a in (1, 2):
                    pool.memset(q_hi[a][:, :, :].bitcast(F32), 0.0).then_inc(s_zeros, 1)
                    pool.memset(q_lo[a][:, :, :].bitcast(F32), 0.0).then_inc(s_zeros, 1)
                x_power(0)

            def x_power(batch):
                pool.wait_ge(s_x_var, batch + 1)
                pool.tensor_tensor(x_rstd[:, :], x_var[:, :], neg_half[:, :], ALU.pow).then_inc(s_x_rstd, 1)

            def residual(h):
                pool.wait_ge(s_rows, (h.pos + 1) * PAIRS)
                pool.wait_ge(s_inv, h.pos + 1)
                if h.att == 2:
                    pool.wait_ge(s_pe_again, (h.batch + 1) * 16)
                src = pe_again if h.att == 2 else pe[h.par]
                for t in range(NT):
                    r = rows[h.att][:, :, t * P:(t + 1) * P]
                    heads = r.rearrange("p c (a d) -> p c a d", a=2)
                    inv = inv_sums[:, t, :].rearrange("p (c a) -> p c a", a=2).unsqueeze(3)\
                        .to_broadcast([P, PAIRS, 2, HD])
                    pool.tensor_tensor(heads, heads, inv, ALU.mult).then_inc(s_res_step, 1)
                for t in range(NT):
                    r = rows[h.att][:, :, t * P:(t + 1) * P]
                    add = src[:, t, :].rearrange("p (c n) -> p c n", c=PAIRS)
                    pool.wait_ge(s_res_step, 4 * h.pos + t + 1)
                    pool.tensor_tensor(r, r, add, ALU.add).then_inc(s_res_step, 1)
                for t in range(NT):
                    r = rows[h.att][:, :, t * P:(t + 1) * P]
                    bias = bv_row[h.att][:, :].rearrange("p (c n) -> p c n", c=PAIRS)
                    pool.wait_ge(s_res_step, 4 * h.pos + NT + t + 1)
                    add = pool.tensor_tensor(r, r, bias, ALU.add)
                add.then_inc(s_res, 1)

            def row_power(h):
                pool.wait_ge(s_row_var, h.pos + 1)
                pool.tensor_tensor(row_rstd[:, :], row_var[:, :], neg_half[:, :], ALU.pow).then_inc(s_row_rstd, 1)

            def project(side):
                if side.att == 2:
                    build_mask(2, B - 1, H * (2 * B - 1))

            def half(h):
                if h.side is not None:
                    if h.att == 2:
                        build_mask(1, h.batch + 2, h.head0)
                    else:
                        build_mask(2, h.batch - 1, h.head0)
                if h.before is not None:
                    residual(h.before)
                if h.att == 1 and h.ahead:
                    x_power(h.batch + 1)
                if h.before is not None:
                    row_power(h.before)

            def drain(h):
                residual(h)
                row_power(h)
                if h.att == 1:
                    build_mask(1, 1, H)

            schedule(setup, project, half, drain, pool.Fori)

        @block.tensor
        def _(pe_eng):
            mm, tr = pe_eng.matmul, pe_eng.transpose

            def three(out, stat_hi, stat_lo, mov_hi, mov_lo, first, last):
                mm(out, stat_hi, mov_hi, start=first, stop=False)
                mm(out, stat_hi, mov_lo, start=False, stop=False)
                return mm(out, stat_lo, mov_hi, start=False, stop=last)

            def group_ready(side, j, m):
                at_least(pe_eng, s_hi, m - 1)
                at_least(pe_eng, s_lo, m - 1)
                if j == 0:
                    if side.att == 1:
                        pe_eng.wait_ge(s_pe, side.batch + 1)
                    elif isinstance(side.batch, int) and side.batch == 0:
                        pe_eng.wait_ge(s_ln, 1)
                    else:
                        pe_eng.wait_ge(s_ln, 2 * side.batch)
                if j == 2:
                    pe_eng.wait_ge(s_hi, side.first + 2)
                    pe_eng.wait_ge(s_lo, side.first + 2)

            def side_piece(side, j, c):
                m, bank = side.first + j, proj_ps[j % 2]
                if c == 0:
                    group_ready(side, j, m)
                last = None
                if j < 2:
                    chunk = 2 * j + c
                    for t in range(NT):
                        src = pe[side.par][:, t, chunk * P:(chunk + 1) * P] if side.att == 1 else \
                            rows[1][:, chunk, t * P:(t + 1) * P]
                        last = tr(bank[:, c * N + t * P:c * N + (t + 1) * P], src, ident[:, :])
                elif j < 6:
                    names = ("n2e_q_w", "n2e_k_w") if side.att == 1 else ("e2n_q_w", "e2n_k_w")
                    name = names[j % 2]
                    edge = side.att == 2 and j % 2 == 1
                    hi, lo = (edge_t_hi, edge_t_lo) if edge else (pe_t_hi[side.par], pe_t_lo[side.par])
                    o = (2 * ((j - 2) // 2) + c) * P
                    for d in range(DC):
                        last = three(bank[:, c * N:(c + 1) * N], w_hi[name][:, d, o:o + P], w_lo[name][:, d, o:o + P],
                                     hi[:, d, :], lo[:, d, :], d == 0, d == DC - 1)
                else:
                    name = "n2e_v_w" if side.att == 1 else "e2n_v_w"
                    hi, lo = (edge_t_hi, edge_t_lo) if side.att == 2 else (pe_t_hi[side.par], pe_t_lo[side.par])
                    t = j - 6
                    for d in range(2 * c, 2 * c + 2):
                        last = three(bank[:, :], hi[:, d, t * P:(t + 1) * P], lo[:, d, t * P:(t + 1) * P],
                                     w_hi[name][:, d, :], w_lo[name][:, d, :], d == 0, d == DC - 1)
                if c == 1:
                    last.then_inc(s_group, 1)

            def scores(h, u):
                g = h.head0 + u
                if u == 0:
                    first = Side(h.att, h.batch, h.par).first
                    pe_eng.wait_ge(s_hi, first + 6)
                    pe_eng.wait_ge(s_lo, first + 6)
                at_least(pe_eng, s_exp, g - 1)
                for t in range(NT):
                    q = (slice(None), u, slice(t * P, (t + 1) * P))
                    last = three(scores_ps[u % 2][:, t * N:(t + 1) * N], q_hi[h.att][q], q_lo[h.att][q],
                                 k_hi[h.att][:, u // 2, :], k_lo[h.att][:, u // 2, :], True, True)
                last.then_inc(s_scores, 1)

            def transpose_probs(h, u):
                g = h.head0 + u
                pe_eng.wait_ge(s_exp, g + 1)
                for j in range(NT):
                    for t in range(NT):
                        last = tr(probs_t_ps[u % 2][:, j * N + t * P:j * N + (t + 1) * P],
                                  probs[:, t, j * P:(j + 1) * P], ident[:, :])
                last.then_inc(s_probs_t, 1)

            def weigh_values(h, u):
                g = h.head0 + u
                if u == 0:
                    first = Side(h.att, h.batch, h.par).first
                    pe_eng.wait_ge(s_hi, first + GROUPS)
                    pe_eng.wait_ge(s_lo, first + GROUPS)
                if u % 2 == 0:
                    at_least(pe_eng, s_heads_t, h.pos * PAIRS + u // 2)
                pe_eng.wait_ge(s_pt_hi, g + 1)
                pe_eng.wait_ge(s_pt_lo, g + 1)
                out = heads_ps[:, (u % 2) * N:(u % 2 + 1) * N]
                for j in range(NT):
                    mm(out, v_both[h.att][:, j, u, :], probs_t_hi[:, j, :], start=j == 0, stop=False)
                    last = mm(out, v_both[h.att][:, j, u, :], probs_t_lo[:, j, :], start=False, stop=j == NT - 1)
                last.then_inc(s_pv, 1)

            def transpose_heads(h, p):
                pair = h.pos * PAIRS + p
                pe_eng.wait_ge(s_heads_t, pair + 1)
                at_least(pe_eng, s_rows, pair)
                for t in range(NT):
                    for a in range(2):
                        o = (t * 2 + a) * P
                        last = tr(rows_ps[:, o:o + P], heads_t[:, a, t * P:(t + 1) * P], ident[:, :])
                last.then_inc(s_rows_ps, 1)

            def setup():
                pe_eng.wait_ge(s_consts, 2)
                for n in range(HALVES - 4, HALVES):
                    pe_eng.wait_ge(s_stage[n % 2], 16 * (n // 2 + 1))
                    raw = stage[n % 2]
                    if n < HALVES - 2:
                        pe_eng.wait_ge(s_vectors, 16 * (len(COLUMN_VECTORS) + 2))
                        for o in range(DC):
                            for c in range(CH):
                                d = CH * (n % 2) + c
                                last = mm(scores_ps[n % 2][:, o:o + 1], raw[:, c, o * P:(o + 1) * P],
                                          col["norm1_b"][:, d:d + 1], start=c == 0, stop=c == CH - 1)
                    else:
                        pe_eng.wait_ge(s_b_bcast, 1)
                        for c in range(CH):
                            d = CH * (n % 2) + c
                            last = mm(heads_ps[:, :], probs[:, :, :].rearrange("p t n -> p (t n)")[:, d * P:(d + 1) * P],
                                      raw[:, c, :], start=d == 0, stop=d == DC - 1)
                    last.then_inc(s_w_bias, 1)
                pe_eng.wait_ge(s_w_hi, HALVES)
                pe_eng.wait_ge(s_w_lo, HALVES)
                pe_eng.wait_ge(s_zeros, 4)
                pe_eng.wait_ge(s_biases, 2)

            def project(side):
                for j in range(GROUPS):
                    side_piece(side, j, 0)
                    side_piece(side, j, 1)

            def half(h):
                for u in range(H):
                    scores(h, u)
                    if h.side is not None:
                        if u == 0:
                            side_piece(h.side, 0, 0)
                            side_piece(h.side, 0, 1)
                        elif u < 7:
                            side_piece(h.side, u + 1, 0)
                    if u == 1 and h.before is not None:
                        transpose_heads(h.before, PAIRS - 1)
                    if u >= 3 and u % 2 == 1:
                        transpose_heads(h, (u - 3) // 2)
                    if u:
                        transpose_probs(h, u - 1)
                    elif h.before is not None:
                        transpose_probs(h.before, H - 1)
                    if h.side is not None:
                        if u == 0:
                            side_piece(h.side, 1, 0)
                            side_piece(h.side, 1, 1)
                        elif u < 7:
                            side_piece(h.side, u + 1, 1)
                    if u:
                        weigh_values(h, u - 1)
                    elif h.before is not None:
                        weigh_values(h.before, H - 1)

            def drain(h):
                transpose_probs(h, H - 1)
                weigh_values(h, H - 1)
                transpose_heads(h, PAIRS - 1)

            schedule(setup, project, half, drain, pe_eng.Fori)

        @block.scalar
        def _(act):
            def project_hi(side, j):
                m, bank = side.first + j, proj_ps[j % 2]
                act.wait_ge(s_group, m + 1)
                if j < 2:
                    dst = pe_t_hi[side.par] if side.att == 1 else edge_t_hi
                    act.activation(dst[:, 2 * j:2 * j + 2, :].rearrange("p c n -> p (c n)"), bank[:, :], ACT.Copy)\
                        .then_inc(s_hi, 1)
                elif j < 6:
                    pair0 = 2 * ((j - 2) // 2)
                    for c in range(2):
                        src, ch = bank[:, c * N:(c + 1) * N], pair0 + c
                        if j % 2:
                            bias = col["n2e_k_b" if side.att == 1 else "e2n_k_b"]
                            last = act.activation(k_hi[side.att][:, ch, :], src, ACT.Identity, bias=bias[:, ch:ch + 1])
                        else:
                            bias = col["n2e_q_b" if side.att == 1 else "e2n_q_b"]
                            for a in range(2):
                                s = slice(a * HD, (a + 1) * HD)
                                last = act.activation(q_hi[side.att][s, 2 * ch + a, :], src[s, :], ACT.Identity,
                                                      bias=bias[s, ch:ch + 1])
                    last.then_inc(s_hi, 1)
                else:
                    t = j - 6
                    act.activation(v_both[side.att][:, t, :, 0:HD], bank[:, :].rearrange("p (h d) -> p h d", h=H),
                                   ACT.Copy).then_inc(s_hi, 1)

            def exps(h, u):
                g = h.head0 + u
                act.wait_ge(s_max, g + 1)
                at_least(act, s_probs_t, g)
                for t in range(NT):
                    last = act.activation(probs[:, t, :], scores_ps[u % 2][:, t * N:(t + 1) * N], ACT.Exp,
                                          bias=neg_max[:, u % 2, t:t + 1], scale=-1.0,
                                          accum_out=sums[h.att][:, t, u:u + 1])
                last.then_inc(s_exp, 1)

            def probs_hi(h, u):
                g = h.head0 + u
                act.wait_ge(s_probs_t, g + 1)
                at_least(act, s_pv, g)
                act.activation(probs_t_hi[:, :, :].rearrange("p t n -> p (t n)"), probs_t_ps[u % 2][:, :], ACT.Copy)\
                    .then_inc(s_pt_hi, 1)

            def heads_out(h, p):
                pair = h.pos * PAIRS + p
                act.wait_ge(s_pv, h.head0 + 2 * p + 2)
                at_least(act, s_rows_ps, pair)
                act.activation(heads_t[:, :, :].rearrange("p a n -> p (a n)"), heads_ps[:, :], ACT.Copy)\
                    .then_inc(s_heads_t, 1)

            def x_relu(batch, par):
                act.wait_ge(s_x_shift, batch + 1)
                for t in range(NT):
                    last = act.activation(pe[par][:, t, :], pe[par][:, t, :], ACT.Relu,
                                          bias=x_shift[:, t:t + 1], scale=x_rstd[:, t:t + 1])
                last.then_inc(s_pe, 1)

            def setup():
                for n in range(HALVES):
                    name = WEIGHTS[n // 2]
                    if n < HALVES - 4:
                        act.wait_ge(s_stage[n % 2], 16 * (n // 2 + 1))
                    else:
                        act.wait_ge(s_w_scaled, n - (HALVES - 4) + 1)
                    act.activation(w_hi[name][:, CH * (n % 2):CH * (n % 2) + CH, :], stage[n % 2], ACT.Copy)\
                        .then_inc(s_w_hi, 1)
                    if n == 0:
                        x_relu(0, 0)
                act.wait_ge(s_vectors, 16 * (len(COLUMN_VECTORS) + 2))
                act.wait_ge(s_zeros, 4)
                act.wait_ge(s_biases, 2)

            def project(side):
                for j in range(GROUPS):
                    project_hi(side, j)

            def half(h):
                for u in range(H):
                    if h.side is not None:
                        project_hi(h.side, u) if u != 1 else None
                    exps(h, u)
                    if u:
                        probs_hi(h, u - 1)
                    elif h.before is not None:
                        probs_hi(h.before, H - 1)
                    if u == 0 and h.side is not None:
                        project_hi(h.side, 1)
                    if u % 2 == 0:
                        if u:
                            heads_out(h, u // 2 - 1)
                        elif h.before is not None:
                            heads_out(h.before, PAIRS - 1)
                    if u == 6 and h.att == 1 and h.ahead:
                        x_relu(h.batch + 1, 1 - h.par)

            def drain(h):
                probs_hi(h, H - 1)
                heads_out(h, PAIRS - 1)

            schedule(setup, project, half, drain, act.Fori)

        @block.vector
        def _(dve):
            def project_lo(side, j):
                m, bank = side.first + j, proj_ps[j % 2]
                dve.wait_ge(s_hi, m + 1)
                if j < 2:
                    hi, lo = (pe_t_hi[side.par], pe_t_lo[side.par]) if side.att == 1 else (edge_t_hi, edge_t_lo)
                    s = (slice(None), slice(2 * j, 2 * j + 2), slice(None))
                    dve.tensor_tensor(lo[s].rearrange("p c n -> p (c n)"), bank[:, :],
                                      hi[s].rearrange("p c n -> p (c n)").bitcast(F32), ALU.subtract).then_inc(s_lo, 1)
                elif j < 6:
                    pair0 = 2 * ((j - 2) // 2)
                    for c in range(2):
                        src, ch = bank[:, c * N:(c + 1) * N], pair0 + c
                        if j % 2:
                            bias = col["n2e_k_b" if side.att == 1 else "e2n_k_b"]
                            last = dve.scalar_tensor_tensor(k_lo[side.att][:, ch, :], src, bias[:, ch:ch + 1],
                                                            k_hi[side.att][:, ch, :].bitcast(F32), ALU.add, ALU.subtract)
                        else:
                            bias = col["n2e_q_b" if side.att == 1 else "e2n_q_b"]
                            for a in range(2):
                                s = slice(a * HD, (a + 1) * HD)
                                last = dve.scalar_tensor_tensor(
                                    q_lo[side.att][s, 2 * ch + a, :], src[s, :], bias[s, ch:ch + 1],
                                    q_hi[side.att][s, 2 * ch + a, :].bitcast(F32), ALU.add, ALU.subtract)
                    last.then_inc(s_lo, 1)
                else:
                    t = j - 6
                    v = v_both[side.att]
                    dve.tensor_tensor(v[:, t, :, HD:P], bank[:, :].rearrange("p (h d) -> p h d", h=H),
                                      v[:, t, :, 0:HD].bitcast(F32), ALU.subtract).then_inc(s_lo, 1)

            def maxima(h, u):
                g = h.head0 + u
                if u == 0:
                    dve.wait_ge(s_mask, mask_number(h.att, h.batch) + 1)
                dve.wait_ge(s_scores, g + 1)
                hold(dve, s_passed["dve"])
                for t in range(NT):
                    s = scores_ps[u % 2][:, t * N:(t + 1) * N]
                    last = dve.tensor_tensor_reduce(s, s, mask[h.att][:, t, :], -SCALE, 3e38, ALU.add, ALU.min,
                                                    neg_max[:, u % 2, t:t + 1])
                last.then_inc(s_max, 1)

            def probs_lo(h, u):
                g = h.head0 + u
                dve.wait_ge(s_pt_hi, g + 1)
                dve.tensor_tensor(probs_t_lo[:, :, :].rearrange("p t n -> p (t n)"), probs_t_ps[u % 2][:, :],
                                  probs_t_hi[:, :, :].rearrange("p t n -> p (t n)").bitcast(F32), ALU.subtract)\
                    .then_inc(s_pt_lo, 1)

            def head_rows(h, p):
                pair = h.pos * PAIRS + p
                if p == 0 and h.att == 2:
                    dve.wait_ge(s_pe_again, (h.batch + 1) * 16)
                dve.wait_ge(s_rows_ps, pair + 1)
                dve.tensor_reduce(rows[h.att][:, p, :].rearrange("p (a d) -> p a d", a=4),
                                  rows_ps[:, :].rearrange("p (a x d) -> p a d x", a=4, x=2), AX_X, ALU.add)\
                    .then_inc(s_rows, 1)

            def inverse_sums(h):
                dve.wait_ge(s_exp, h.head0 + H)
                dve.reciprocal(inv_sums[:, :, :].rearrange("p t h -> p (t h)"),
                               sums[h.att][:, :, :].rearrange("p t h -> p (t h)")).then_inc(s_inv, 1)

            def moments(src, stats, mv, var, s_stats, s_var, count):
                for t in range(NT):
                    dve.bn_stats(stats[:, t, :], src(t)).then_inc(s_stats, 1)
                for t in range(NT):
                    dve.wait_ge(s_stats, count * 2 * NT + t + 1)
                    hold(dve, s_passed["dve"])
                    dve.bn_aggr(mv[:, t, :], stats[:, t, :]).then_inc(s_stats, 1)
                dve.wait_ge(s_stats, count * 2 * NT + 2 * NT)
                dve.tensor_scalar(var[:, :], mv[:, :, 1], LN_EPS, None, ALU.add).then_inc(s_var, 1)

            def x_moments(batch, par):
                dve.wait_ge(s_x, (batch + 1) * 16)
                moments(lambda t: pe[par][:, t, :], x_stats, x_mv, x_var, s_x_stats, s_x_var, batch)

            def x_shifts(batch):
                dve.wait_ge(s_x_rstd, batch + 1)
                dve.scalar_tensor_tensor(x_shift[:, :], x_mv[:, :, 0], -1.0, x_rstd[:, :], ALU.mult, ALU.mult)\
                    .then_inc(s_x_shift, 1)

            def row_moments(h):
                dve.wait_ge(s_res, h.pos + 1)
                moments(lambda t: rows[h.att][:, :, t * P:(t + 1) * P], row_stats, row_mv, row_var,
                        s_row_stats, s_row_var, h.pos)

            def normalise(h):
                dve.wait_ge(s_row_rstd, h.pos + 1)
                for t in range(NT):
                    r = rows[h.att][:, :, t * P:(t + 1) * P]
                    last = dve.tensor_scalar(r, r, row_mv[:, t, 0:1], row_rstd[:, t:t + 1], ALU.subtract, ALU.mult)
                last.then_inc(s_ln, 1)

            def setup():
                dve.wait_ge(s_vectors, 16 * (len(COLUMN_VECTORS) + 2))
                x_moments(0, 0)
                x_shifts(0)
                for c in range(DC):
                    last = dve.tensor_copy(probs[:, :, :].rearrange("p t n -> p (t n)")[:, c * P:(c + 1) * P],
                                           col["norm1_b"][:, c:c + 1].to_broadcast([P, P]))
                last.then_inc(s_b_bcast, 1)
                for n in range(HALVES):
                    name = WEIGHTS[n // 2]
                    if n >= HALVES - 4:
                        k = n - (HALVES - 4)
                        dve.wait_ge(s_stage[n % 2], 16 * (n // 2 + 1))
                        dve.wait_ge(s_w_bias, k + 1)
                        for c in range(CH):
                            d = CH * (n % 2) + c
                            last = dve.tensor_scalar(stage[n % 2][:, c, :], stage[n % 2][:, c, :],
                                                     col["norm1_g"][:, d:d + 1], None, ALU.mult)
                        last.then_inc(s_w_scaled, 1)
                    dve.wait_ge(s_w_hi, n + 1)
                    s = (slice(None), slice(CH * (n % 2), CH * (n % 2) + CH), slice(None))
                    dve.tensor_tensor(w_lo[name][s], stage[n % 2], w_hi[name][s].bitcast(F32), ALU.subtract)\
                        .then_inc(s_w_lo, 1)
                dve.tensor_copy(bias_parts[:, 0:DC], scores_ps[0][:, 0:DC]).then_inc(s_biases, 1)
                dve.wait_ge(s_biases, 1)
                dve.tensor_tensor(bias_parts[:, DC:2 * DC], scores_ps[1][:, 0:DC], bias_parts[:, 0:DC], ALU.add)\
                    .then_inc(s_b_bcast, 1)
                dve.wait_ge(s_b_bcast, 2)
                dve.tensor_tensor(col["e2n_k_b"][:, :], col["e2n_k_b"][:, :], bias_parts[:, DC:2 * DC], ALU.add)\
                    .then_inc(s_b_bcast, 1)
                dve.tensor_tensor(bv_row[2][:, :], heads_ps[:, :], bv_row[2][:, :], ALU.add).then_inc(s_b_bcast, 1)
                dve.wait_ge(s_b_bcast, 4)
                dve.tensor_copy(bias_parts[:, 0:1], neg_half[:, 0:1]).then_inc(s_biases, 1)

            def project(side):
                for j in range(GROUPS):
                    project_lo(side, j)

            def half(h):
                for u in range(H):
                    if u == 0 and h.side is not None:
                        project_lo(h.side, 0)
                    maxima(h, u)
                    if u > 1 and h.side is not None:
                        project_lo(h.side, u)
                    if u:
                        probs_lo(h, u - 1)
                    elif h.before is not None:
                        probs_lo(h.before, H - 1)
                    if u == 0 and h.side is not None:
                        project_lo(h.side, 1)
                    if u == 1 and h.before is not None:
                        inverse_sums(h.before)
                        head_rows(h.before, PAIRS - 1)
                    if u >= 3 and u % 2 == 1:
                        head_rows(h, (u - 3) // 2)
                    if h.att == 1 and h.ahead:
                        if u == 2:
                            x_moments(h.batch + 1, 1 - h.par)
                        if u == 5:
                            x_shifts(h.batch + 1)
                    if h.before is not None:
                        if u == 5:
                            row_moments(h.before)
                        if u == 6:
                            normalise(h.before)

            def drain(h):
                probs_lo(h, H - 1)
                inverse_sums(h)
                head_rows(h, PAIRS - 1)
                row_moments(h)
                normalise(h)

            schedule(setup, project, half, drain, dve.Fori)


def feed_forward_part(nc, x, node_rows, w1, w2, gain2_col, bias2_col, b1_col, row_vectors, out):
    with ExitStack() as ctx:
        def sb(name, shape, dt=F32):
            return ctx.enter_context(nc.sbuf_tensor(name, shape, dt))

        def ps(name):
            return ctx.enter_context(nc.psum_tensor(name, [P, 512], F32))

        def sem(name):
            return ctx.enter_context(nc.semaphore(name))

        w1_hi, w1_lo = sb("w1_hi", [P, DC, FF], F32R), sb("w1_lo", [P, DC, FF], F32R)
        w2_hi, w2_lo = sb("w2_hi", [P, FT, D], F32R), sb("w2_lo", [P, FT, D], F32R)
        z = [sb(f"z{i}", [P, RT, D]) for i in range(2)]
        xr = [sb(f"xr{i}", [P, RT, D]) for i in range(2)]
        z_t_hi, z_t_lo = sb("z_t_hi", [P, DC, ROWS], F32R), sb("z_t_lo", [P, DC, ROWS], F32R)
        hid = [sb(f"hid{i}", [P, ROWS]) for i in range(2)]
        hid_hi = [sb(f"hid_hi{i}", [P, ROWS], F32R) for i in range(2)]
        hid_lo = [sb(f"hid_lo{i}", [P, ROWS], F32R) for i in range(2)]
        gain2, bias2, gain3, bias3, b2_row = (sb(n, [P, D]) for n in ("gain2", "bias2", "gain3", "bias3", "b2_row"))
        gain2_c, bias2_c, b1_c = sb("gain2_c", [P, DC]), sb("bias2_c", [P, DC]), sb("b1_c", [P, FT])
        ident2 = sb("ident2", [P, P])
        neg_half2 = sb("neg_half2", [P, RT])
        stats, mv = sb("stats", [P, RT, BN_S]), sb("mv", [P, RT, BN_A])
        var, rstd = sb("var", [P, RT]), sb("rstd", [P, RT])

        hid_ps = [ps(f"hid_ps{i}") for i in range(2)]
        t_ps = [ps(f"t_ps{i}") for i in range(2)]
        out_ps = [ps(f"out_ps{i}") for i in range(RT)]

        f_passed = {e: sem(f"ff_passed_{e}") for e in ("sp", "dve")}
        f_vec = sem("ff_vectors_loaded")
        f_const = sem("ff_constants")
        f_stage = [sem(f"ff_staged{i}") for i in range(2)]
        f_w_scaled = sem("ff_scaled")
        f_w_hi = sem("ff_weights_hi")
        f_w_lo = sem("ff_weights_lo")
        f_w_bias = sem("ff_bias_products")
        f_b1 = sem("ff_b1_ready")
        f_b2 = sem("ff_b2_ready")
        f_z = [sem(f"z_loaded{i}") for i in range(2)]
        f_x = [sem(f"x_again_loaded{i}") for i in range(2)]
        f_t = sem("z_transposed")
        f_t_hi = sem("z_t_hi_ready")
        f_t_lo = sem("z_t_lo_ready")
        f_hid_ps = sem("hid_done")
        f_hid = sem("gelu_ready")
        f_hid_hi = sem("hid_hi_ready")
        f_hid_lo = sem("hid_lo_ready")
        f_hid_used = sem("hid_used")
        f_node_step = sem("node_step")
        f_node = sem("node_features_ready")
        f_x_bias = sem("x_biased")
        f_out_ps = sem("out_done")
        f_sum = sem("sum_ready")
        f_stats = sem("ff_stats")
        f_var = sem("ff_var")
        f_rstd = sem("ff_rstd")
        f_norm = sem("ff_normalised")
        f_gain = sem("ff_gain")
        f_final = sem("ff_final")
        f_stored = [sem(f"out_stored{i}") for i in range(2)]

        STAGES = 2 * DC

        def stage_of(n):
            return z[n % 2][:, :, :].rearrange("p t d -> p (t d)")

        def weight_part(n, one, two):
            if n < DC:
                return one[:, n, :]
            q = FT // DC
            return two[:, (n - DC) * q:(n - DC + 1) * q, :].rearrange("p f d -> p (f d)")

        def schedule(do_setup, do_pass, loop):
            do_setup()
            do_pass(0, 0, 0)
            do_pass(1, 1, 0)
            with loop(1, PASSES // 2 - 1) as i:
                do_pass(2 * i, 0, i)
                do_pass(2 * i + 1, 1, i)
            do_pass(PASSES - 2, 0, PASSES // 2 - 1)
            do_pass(PASSES - 1, 1, PASSES // 2 - 1, last=True)

        block = ctx.enter_context(nc.Block())

        @block.sync
        def _(sp):
            def load(dst, src, r, s):
                hold(sp, f_passed["sp"])
                sp.dma_start(dst[:, :, :], src[bass.ds(r * ROWS, ROWS), :].rearrange(
                    "(t p) d -> p t d", p=P)).then_inc(s, 16)

            def setup():
                for dst, src in ((gain2_c, gain2_col), (bias2_c, bias2_col), (b1_c, b1_col)):
                    sp.dma_start(dst[:, :], src).then_inc(f_vec, 16)
                for dst, src in zip((gain2, bias2, gain3, bias3, b2_row), row_vectors):
                    sp.dma_start(dst[:, :], src.to_broadcast([P, D])).then_inc(f_vec, 16)
                for n in range(STAGES):
                    if n >= 2:
                        sp.wait_ge(f_w_hi, n - 1)
                        hold(sp, f_passed["sp"])
                        sp.wait_ge(f_w_lo, n - 1)
                        hold(sp, f_passed["sp"])
                    src = w1[n * P:(n + 1) * P, :] if n < DC else \
                        w2[(n - DC) * D:(n - DC + 1) * D, :].rearrange("(f p) d -> p f d", p=P)
                    dst = z[n % 2][:, :, :].rearrange("p t d -> p (t d)") if n < DC else z[n % 2][:, :, :]
                    sp.dma_start(dst, src).then_inc(f_stage[n % 2], 16)
                sp.wait_ge(f_w_hi, STAGES)
                hold(sp, f_passed["sp"])
                sp.wait_ge(f_w_lo, STAGES)
                hold(sp, f_passed["sp"])
                load(z[0], node_rows, 0, f_z[0])
                load(xr[0], x, 0, f_x[0])

            def do_pass(r, par, i, last=False):
                if not last:
                    nxt = 1 - par
                    if not (isinstance(r, int) and r == 0):
                        sp.wait_ge(f_final, r * RT)
                        hold(sp, f_passed["sp"])
                        sp.wait_ge(f_stored[nxt], (i + par) * RT * 16)
                        hold(sp, f_passed["sp"])
                    load(z[nxt], node_rows, r + 1, f_z[nxt])
                    load(xr[nxt], x, r + 1, f_x[nxt])
                for t in range(RT):
                    sp.wait_ge(f_final, r * RT + t + 1)
                    hold(sp, f_passed["sp"])
                    sp.dma_start(out[bass.ds(r * ROWS + t * P, P), :], xr[par][:, t, :]).then_inc(f_stored[par], 16)
                if isinstance(r, int) and r >= PASSES - 2:
                    sp.wait_ge(f_stored[par], (i + 1) * RT * 16)
                    hold(sp, f_passed["sp"])

            schedule(setup, do_pass, sp.Fori)

        @block.gpsimd
        def _(pool):
            def setup():
                pool.memset(ident2[:, :], 0.0).then_inc(f_const, 1)
                pool.wait_ge(f_const, 1)
                pool.affine_select(out=ident2[:, :], in_=ident2[:, :], compare_op=ALU.not_equal, fill=1.0,
                                   base=0, pattern=[[-1, P]], channel_multiplier=1).then_inc(f_const, 1)
                pool.memset(neg_half2[:, :], -0.5).then_inc(f_const, 1)
                pool.wait_ge(f_vec, 16 * 8)
                pool.tensor_tensor(bias2[:, :], bias2[:, :], b2_row[:, :], ALU.add).then_inc(f_b2, 1)
                pool.wait_ge(f_b2, 1)
                pool.wait_ge(f_const, 3)

            def finish(r, par):
                for t in range(RT):
                    pool.wait_ge(f_norm, r * RT + t + 1)
                    pool.tensor_tensor(z[par][:, t, :], z[par][:, t, :], gain3[:, :], ALU.mult).then_inc(f_gain, 1)
                for t in range(RT):
                    pool.wait_ge(f_gain, r * RT + t + 1)
                    pool.tensor_tensor(xr[par][:, t, :], xr[par][:, t, :], z[par][:, t, :], ALU.add)\
                        .then_inc(f_final, 1)

            def power(r):
                pool.wait_ge(f_var, r + 1)
                pool.tensor_tensor(rstd[:, :], var[:, :], neg_half2[:, :], ALU.pow).then_inc(f_rstd, 1)

            def do_pass(r, par, i, last=False):
                if not (isinstance(r, int) and r == 0):
                    power(r - 1)
                    finish(r - 1, 1 - par)
                pool.wait_ge(f_x[par], (i + 1) * 16)
                for t in range(RT):
                    pool.tensor_tensor(xr[par][:, t, :], xr[par][:, t, :], bias3[:, :], ALU.add).then_inc(f_x_bias, 1)
                pool.wait_ge(f_z[par], (i + 1) * 16)
                pool.wait_ge(f_t, r * DC + DC)
                for t in range(RT):
                    pool.tensor_tensor(z[par][:, t, :], z[par][:, t, :], gain2[:, :], ALU.mult).then_inc(f_node_step, 1)
                for t in range(RT):
                    pool.wait_ge(f_node_step, r * RT + t + 1)
                    pool.tensor_tensor(z[par][:, t, :], z[par][:, t, :], bias2[:, :], ALU.add).then_inc(f_node, 1)
                pool.wait_ge(f_x_bias, (r + 1) * RT)
                if last:
                    power(r)
                    finish(r, par)

            schedule(setup, do_pass, pool.Fori)

        @block.tensor
        def _(pe_eng):
            mm, tr = pe_eng.matmul, pe_eng.transpose

            def transpose_rows(r, par, i, c):
                if c == 0:
                    pe_eng.wait_ge(f_z[par], (i + 1) * 16)
                if not (isinstance(r, int) and r == 0 and c < 2):
                    pe_eng.wait_ge(f_t_hi, r * DC + c - 1)
                    pe_eng.wait_ge(f_t_lo, r * DC + c - 1)
                for t in range(RT):
                    last = tr(t_ps[c % 2][:, t * P:(t + 1) * P], z[par][:, t, c * P:(c + 1) * P], ident2[:, :])
                last.then_inc(f_t, 1)

            def hidden(r, f):
                n = r * FT + f
                if f == 0:
                    pe_eng.wait_ge(f_t_hi, (r + 1) * DC)
                    pe_eng.wait_ge(f_t_lo, (r + 1) * DC)
                if not (isinstance(r, int) and r == 0 and f < 2):
                    pe_eng.wait_ge(f_hid, n - 1)
                o = hid_ps[f % 2][:, :]
                s = slice(f * P, (f + 1) * P)
                for d in range(DC):
                    mm(o, w1_hi[:, d, s], z_t_hi[:, d, :], start=d == 0, stop=False)
                    mm(o, w1_hi[:, d, s], z_t_lo[:, d, :], start=False, stop=False)
                    last = mm(o, w1_lo[:, d, s], z_t_hi[:, d, :], start=False, stop=d == DC - 1)
                last.then_inc(f_hid_ps, 1)

            def outcome(r, f):
                n = r * FT + f
                pe_eng.wait_ge(f_hid_hi, n + 1)
                pe_eng.wait_ge(f_hid_lo, n + 1)
                for t in range(RT):
                    if f == 0 and not (isinstance(r, int) and r == 0):
                        pe_eng.wait_ge(f_sum, (r - 1) * RT + t + 1)
                    s = slice(t * P, (t + 1) * P)
                    o = out_ps[t][:, :]
                    mm(o, hid_hi[f % 2][:, s], w2_hi[:, f, :], start=f == 0, stop=False)
                    mm(o, hid_hi[f % 2][:, s], w2_lo[:, f, :], start=False, stop=False)
                    last = mm(o, hid_lo[f % 2][:, s], w2_hi[:, f, :], start=False, stop=f == FT - 1)
                    if f == FT - 1:
                        last.then_inc(f_out_ps, 1)
                        last = None
                if last is not None:
                    last.then_inc(f_hid_used, 1)

            def setup():
                pe_eng.wait_ge(f_vec, 16 * 8)
                for n in range(DC):
                    pe_eng.wait_ge(f_stage[n % 2], 16 * (n // 2 + 1))
                    for f in range(FT):
                        last = mm(hid_ps[0][:, n * FT + f:n * FT + f + 1], stage_of(n)[:, f * P:(f + 1) * P],
                                  bias2_c[:, n:n + 1], start=True, stop=True)
                    last.then_inc(f_w_bias, 1)
                pe_eng.wait_ge(f_const, 2)
                pe_eng.wait_ge(f_w_hi, STAGES)
                pe_eng.wait_ge(f_w_lo, STAGES)
                pe_eng.wait_ge(f_b1, 4)
                for c in range(DC):
                    transpose_rows(0, 0, 0, c)

            def do_pass(r, par, i, last=False):
                for f in range(FT):
                    hidden(r, f)
                    if f == FT - 1 and not last:
                        transpose_rows(r + 1, 1 - par, i + par, 0)
                        transpose_rows(r + 1, 1 - par, i + par, 1)
                    if f:
                        outcome(r, f - 1)
                if not last:
                    transpose_rows(r + 1, 1 - par, i + par, 2)
                    transpose_rows(r + 1, 1 - par, i + par, 3)
                outcome(r, FT - 1)

            schedule(setup, do_pass, pe_eng.Fori)

        @block.scalar
        def _(act):
            def rows_hi(r, c):
                act.wait_ge(f_t, r * DC + c + 1)
                act.activation(z_t_hi[:, c, :], t_ps[c % 2][:, :], ACT.Copy).then_inc(f_t_hi, 1)

            def setup():
                for n in range(STAGES):
                    if n < DC:
                        act.wait_ge(f_w_scaled, n + 1)
                    else:
                        act.wait_ge(f_stage[n % 2], 16 * (n // 2 + 1))
                    act.activation(weight_part(n, w1_hi, w2_hi), stage_of(n), ACT.Copy).then_inc(f_w_hi, 1)
                act.wait_ge(f_b1, 4)
                for c in range(DC):
                    rows_hi(0, c)

            def do_pass(r, par, i, last=False):
                for f in range(FT):
                    n = r * FT + f
                    act.wait_ge(f_hid_ps, n + 1)
                    if not (isinstance(r, int) and r == 0 and f < 2):
                        act.wait_ge(f_hid_lo, n - 1)
                    act.activation(hid[f % 2][:, :], hid_ps[f % 2][:, :], ACT.Gelu, bias=b1_c[:, f:f + 1])\
                        .then_inc(f_hid, 1)
                if not last:
                    for c in range(DC):
                        rows_hi(r + 1, c)

            schedule(setup, do_pass, act.Fori)

        @block.vector
        def _(dve):
            def rows_lo(r, c):
                dve.wait_ge(f_t_hi, r * DC + c + 1)
                dve.tensor_tensor(z_t_lo[:, c, :], t_ps[c % 2][:, :], z_t_hi[:, c, :].bitcast(F32), ALU.subtract)\
                    .then_inc(f_t_lo, 1)

            def setup():
                dve.wait_ge(f_vec, 16 * 8)
                for n in range(STAGES):
                    if n < DC:
                        dve.wait_ge(f_stage[n % 2], 16 * (n // 2 + 1))
                        dve.wait_ge(f_w_bias, n + 1)
                        dve.tensor_scalar(stage_of(n), stage_of(n), gain2_c[:, n:n + 1], None, ALU.mult)\
                            .then_inc(f_w_scaled, 1)
                    dve.wait_ge(f_w_hi, n + 1)
                    dve.tensor_tensor(weight_part(n, w1_lo, w2_lo), stage_of(n),
                                      weight_part(n, w1_hi, w2_hi).bitcast(F32), ALU.subtract).then_inc(f_w_lo, 1)
                for n in range(DC):
                    if n:
                        dve.wait_ge(f_b1, n)
                    dve.tensor_tensor(b1_c[:, :], hid_ps[0][:, n * FT:(n + 1) * FT], b1_c[:, :], ALU.add)\
                        .then_inc(f_b1, 1)
                for c in range(DC):
                    rows_lo(0, c)

            def split(r, f):
                n = r * FT + f
                dve.wait_ge(f_hid, n + 1)
                if not (isinstance(r, int) and r == 0 and f < 2):
                    if f >= 2:
                        dve.wait_ge(f_hid_used, r * (FT - 1) + f - 1)
                    elif f == 1:
                        dve.wait_ge(f_out_ps, r * RT)
                    else:
                        dve.wait_ge(f_hid_used, r * (FT - 1))
                dve.tensor_copy(hid_hi[f % 2][:, :], hid[f % 2][:, :]).then_inc(f_hid_hi, 1)
                dve.wait_ge(f_hid_hi, n + 1)
                dve.tensor_tensor(hid_lo[f % 2][:, :], hid[f % 2][:, :], hid_hi[f % 2][:, :].bitcast(F32), ALU.subtract)\
                    .then_inc(f_hid_lo, 1)

            def moments(r, par):
                for t in range(RT):
                    dve.wait_ge(f_sum, r * RT + t + 1)
                    dve.bn_stats(stats[:, t, :], z[par][:, t, :]).then_inc(f_stats, 1)

            def spread(r):
                for t in range(RT):
                    dve.wait_ge(f_stats, r * 2 * RT + t + 1)
                    hold(dve, f_passed["dve"])
                    dve.bn_aggr(mv[:, t, :], stats[:, t, :]).then_inc(f_stats, 1)
                dve.wait_ge(f_stats, (r + 1) * 2 * RT)
                dve.tensor_scalar(var[:, :], mv[:, :, 1], LN_EPS, None, ALU.add).then_inc(f_var, 1)

            def normalise(r, par):
                dve.wait_ge(f_rstd, r + 1)
                for t in range(RT):
                    dve.tensor_scalar(z[par][:, t, :], z[par][:, t, :], mv[:, t, 0:1], rstd[:, t:t + 1],
                                      ALU.subtract, ALU.mult).then_inc(f_norm, 1)

            def sums(r, par):
                for t in range(RT):
                    dve.wait_ge(f_out_ps, r * RT + t + 1)
                    dve.wait_ge(f_node, r * RT + t + 1)
                    dve.tensor_tensor(z[par][:, t, :], out_ps[t][:, :], z[par][:, t, :], ALU.add).then_inc(f_sum, 1)

            def do_pass(r, par, i, last=False):
                for f in range(FT):
                    split(r, f)
                    if not (isinstance(r, int) and r == 0):
                        if f == 1:
                            moments(r - 1, 1 - par)
                            spread(r - 1)
                        if f == 3:
                            normalise(r - 1, 1 - par)
                if not last:
                    for c in range(DC):
                        rows_lo(r + 1, c)
                sums(r, par)
                if last:
                    moments(r, par)
                    spread(r)
                    normalise(r, par)

            schedule(setup, do_pass, dve.Fori)


def kernel(**inputs):
    import numpy as np
    import concourse.bacc as bacc
    from concourse.bass_utils import run_bass_kernel_spmd

    nc = bacc.Bacc("TRN2", target_bir_lowering=False, num_devices=1, dynamic_dma_scratch_size=1024)
    arrays = {}

    def given(name, a):
        a = np.ascontiguousarray(a)
        arrays[name] = a
        return nc.dram_tensor(name, a.shape, mybir.dt.from_np(a.dtype), kind="ExternalInput").ap()

    def vector(name):
        return np.asarray(inputs["L0_gnn_" + name])

    def column(name):
        return vector(name).reshape(-1, P).T

    def row(name):
        return given(name + "_row", vector(name).reshape(1, -1))

    x = given("x", np.asarray(inputs["x"]).reshape(B * N, D))
    a = np.asarray(inputs["adj"])
    adj = given("adj", a.reshape(B * N, N))
    adj_t = given("adj_t", a.transpose(0, 2, 1).reshape(B * N, N))
    w = {n: given(n, vector(n).T) for n in WEIGHTS}
    columns = {n: given(n + "_c", column(n)) for n in COLUMN_VECTORS}
    bv1, bv2 = row("n2e_v_b"), row("e2n_v_b")
    w1, w2 = given("ffn_w1", vector("ffn_w1").T), given("ffn_w2", vector("ffn_w2").T)
    gain2_c, bias2_c = given("gain2_in", column("norm2_g")), given("bias2_in", column("norm2_b"))
    b1_c = given("b1_in", column("ffn_b1"))
    row_vectors = [row(n) for n in ("norm2_g", "norm2_b", "norm3_g", "norm3_b", "ffn_b2")]
    pe_rows = nc.dram_tensor("pe_rows", [B * N, D], F32).ap()
    node_rows = nc.dram_tensor("node_rows", [B * N, D], F32).ap()
    out = nc.dram_tensor("out", [B * N, D], F32, kind="ExternalOutput").ap()
    attention_part(nc, x, adj, adj_t, w, columns, bv1, bv2, pe_rows, node_rows)
    feed_forward_part(nc, x, node_rows, w1, w2, gain2_c, bias2_c, b1_c, row_vectors, out)
    r = run_bass_kernel_spmd(nc, [arrays], core_ids=[0])
    return r.results[0]["out"].reshape(B, N, D)
```

```python
from contextlib import ExitStack

import concourse.bass as bass
from concourse import mybir

F32 = mybir.dt.float32
F32R = mybir.dt.float32r
BF16 = mybir.dt.bfloat16
ALU = mybir.AluOpType
ACT = mybir.ActivationFunctionType
AX_X = mybir.AxisListType.X

P = 128
B, N, D, H = 32, 256, 512, 8
HD = D // H
FF = 4 * D
DC = D // P
NT = N // P
PAIRS = H // 2
FT = FF // P
ROWS = 4 * P
RT = ROWS // P
PASSES = B * N // ROWS
SCALE = HD ** -0.5
LN_EPS = 1e-5
MASKED = -1e30
GROUPS = 8
BN_S, BN_A = 6, 2

SIDE_PIECES = [
    ([(0, 0), (0, 1), (1, 0), (1, 1)], []),
    ([(2, 0)], [(2, 1)]),
    ([(3, 0)], [(3, 1)]),
    ([(4, 0)], [(4, 1)]),
    ([(5, 0)], [(5, 1)]),
    ([(6, 0)], [(6, 1)]),
    ([(7, 0)], []),
    ([(7, 1)], []),
]
SIDE_SPLITS = [[0, 1], [], [2], [3], [4], [5], [6], [7]]

SETUP_ORDER = [("w", 0), ("w", 1), ("g", 0), ("g", 1), ("w", 2), ("w", 3), ("g", 2), ("w", 4), ("g", 3), ("w", 5),
               ("g", 4), ("w", 6), ("g", 5), ("w", 7), ("g", 6), ("w", 8), ("g", 7), ("w", 9), ("w", 10), ("w", 11)]

COLUMN_VECTORS = ["n2e_q_b", "n2e_k_b", "e2n_q_b", "e2n_k_b", "norm1_g", "norm1_b"]
WEIGHTS = ["n2e_q_w", "n2e_k_w", "n2e_v_w", "e2n_q_w", "e2n_k_w", "e2n_v_w"]


def hold(engine, passed):
    engine.sem_inc(passed, 1)


def slot_of(att, batch):
    if att == 1 and isinstance(batch, int) and batch == 0:
        return 2
    if att == 2 and isinstance(batch, int) and batch == B - 1:
        return 1
    return att


class Half:

    def __init__(self, att, batch, par, pos, before=None, side=None, ahead=True):
        self.att, self.batch, self.par, self.pos = att, batch, par, pos
        self.before, self.side, self.ahead = before, side, ahead
        self.head0 = pos * H
        self.slot = slot_of(att, batch)
        self.is_first = att == 1 and isinstance(batch, int) and batch == 0
        self.is_second = att == 1 and isinstance(batch, int) and batch == 1
        self.is_last = att == 2 and self.slot == 1


class Side:

    def __init__(self, att, batch, par):
        self.att, self.batch, self.par = att, batch, par
        self.slot = slot_of(att, batch)
        if att == 1:
            self.first = 0 if isinstance(batch, int) and batch == 0 else 2 * GROUPS * batch - GROUPS
        elif isinstance(batch, int) and batch == B - 1:
            self.first = (2 * B - 1) * GROUPS
        else:
            self.first = 2 * GROUPS * batch + 2 * GROUPS


def first_half(k, par, before=True, side=True, ahead=True):
    return Half(1, k, par, 2 * k - 1,
                before=Half(2, k - 2, par, 2 * k - 2) if before else None,
                side=Side(2, k - 1, 1 - par) if side else None, ahead=ahead)


def second_half(k, par, side=True, ahead=True):
    return Half(2, k, par, 2 * k + 2,
                before=Half(1, k + 1, 1 - par, 2 * k + 1),
                side=Side(1, k + 2, par) if side else None, ahead=ahead)


def at_least(engine, semaphore, value):
    if isinstance(value, int) and value <= 0:
        return
    engine.wait_ge(semaphore, value)


def attention_part(nc, x, adj, adj_t, w, columns, bv1_row, bv2_row, peeled_rows, node_rows):
    with ExitStack() as ctx:
        def sb(name, shape, dt=F32):
            return ctx.enter_context(nc.sbuf_tensor(name, shape, dt))

        def ps(name):
            return ctx.enter_context(nc.psum_tensor(name, [P, 512], F32))

        def sem(name):
            return ctx.enter_context(nc.semaphore(name))

        w_hi = {n: sb(f"{n}_hi", [P, DC, D], F32R) for n in WEIGHTS}
        w_lo = {n: sb(f"{n}_lo", [P, DC, D], F32R) for n in WEIGHTS}
        q_hi = {a: sb(f"q{a}_hi", [P, H, N], F32R) for a in (1, 2)}
        q_lo = {a: sb(f"q{a}_lo", [P, H, N], F32R) for a in (1, 2)}
        k_hi = {a: sb(f"k{a}_hi", [P, DC, N], F32R) for a in (1, 2)}
        k_lo = {a: sb(f"k{a}_lo", [P, DC, N], F32R) for a in (1, 2)}
        v_both = {a: sb(f"v{a}", [P, NT, H, P], F32R) for a in (1, 2)}
        pe_t_hi = [sb(f"pe_t_hi{i}", [P, DC, N], F32R) for i in range(2)]
        pe_t_lo = [sb(f"pe_t_lo{i}", [P, DC, N], F32R) for i in range(2)]
        edge_t_hi = sb("edge_t_hi", [P, DC, N], F32R)
        edge_t_lo = sb("edge_t_lo", [P, DC, N], F32R)
        pe = [sb(f"pe{i}", [P, NT, D]) for i in range(2)]
        pe_again = sb("pe_again", [P, NT, D])
        adj_raw = sb("adj_raw", [P, NT, N])
        mask = {a: sb(f"mask{a}", [P, NT, N], BF16) for a in (1, 2)}
        probs = sb("probs", [P, NT, N])
        probs_t_hi = sb("probs_t_hi", [P, NT, N], F32R)
        probs_t_lo = sb("probs_t_lo", [P, NT, N], F32R)
        heads_t = sb("heads_t", [P, 2, N])
        rows = {a: sb(f"rows{a}", [P, PAIRS, NT * P]) for a in (1, 2)}
        bv_row = {a: sb(f"bv{a}_row", [P, D]) for a in (1, 2)}
        col = {n: sb(f"{n}_col", [P, DC]) for n in COLUMN_VECTORS}
        ident = sb("ident", [P, P])
        neg_half = sb("neg_half", [P, NT])
        neg_max = sb("neg_max", [P, 2, NT])
        sums = {a: sb(f"sums{a}", [P, NT, H]) for a in (1, 2)}
        inv_sums = sb("inv_sums", [P, NT, H])
        x_stats, row_stats = sb("x_stats", [P, NT, BN_S]), sb("row_stats", [P, NT, BN_S])
        x_mv, row_mv = sb("x_mv", [P, NT, BN_A]), sb("row_mv", [P, NT, BN_A])
        x_var, row_var = sb("x_var", [P, NT]), sb("row_var", [P, NT])
        x_rstd, row_rstd = sb("x_rstd", [P, NT]), sb("row_rstd", [P, NT])
        x_shift = sb("x_shift", [P, NT])
        bias_parts = sb("bias_parts", [P, 2 * DC])

        scores_ps = [ps(f"scores_ps{i}") for i in range(2)]
        probs_t_ps = [ps(f"probs_t_ps{i}") for i in range(2)]
        proj_ps = [ps(f"proj_ps{i}") for i in range(2)]
        heads_ps = ps("heads_ps")
        rows_ps = ps("rows_ps")

        s_columns = sem("columns_loaded")
        s_bv = sem("value_biases_loaded")
        s_stage = [sem(f"weights_staged{i}") for i in range(2)]
        s_w_hi = sem("weights_hi")
        s_w_lo = sem("weights_lo")
        s_w_scaled = sem("weights_scaled")
        s_w_bias = sem("weight_bias_products")
        s_b_bcast = sem("bias_broadcast")
        s_consts = sem("constants_ready")
        s_zeros = sem("zeros_ready")
        s_biases = sem("biases_ready")
        s_x = sem("x_loaded")
        s_x_stats = sem("x_stats_ready")
        s_x_var = sem("x_var_ready")
        s_x_rstd = sem("x_rstd_ready")
        s_x_shift = sem("x_shift_ready")
        s_pe = sem("pe_ready")
        s_pe_stored = sem("pe_stored")
        s_pe_again = sem("pe_again_loaded")
        s_adj = sem("adj_loaded")
        s_mask = sem("mask_ready")
        s_group = sem("proj_group_done")
        s_hi = sem("proj_hi_ready")
        s_lo = sem("proj_lo_ready")
        s_scores = sem("scores_done")
        s_max = sem("max_ready")
        s_exp = sem("exp_ready")
        s_probs_t = sem("probs_transposed")
        s_pt_hi = sem("probs_t_hi_ready")
        s_pt_lo = sem("probs_t_lo_ready")
        s_pv = sem("values_weighted")
        s_heads_t = sem("heads_t_ready")
        s_rows_ps = sem("rows_transposed")
        s_rows = sem("rows_ready")
        s_inv = sem("inv_sums_ready")
        s_res_step = sem("residual_step")
        s_res = sem("residual_added")
        s_row_stats = sem("row_stats_ready")
        s_row_var = sem("row_var_ready")
        s_row_rstd = sem("row_rstd_ready")
        s_ln = sem("rows_normalised")
        s_node = sem("node_stored")
        s_passed = {e: sem(f"passed_{e}") for e in ("sp", "pool", "dve")}

        HALVES = 2 * len(WEIGHTS)
        CH = DC // 2
        stage = [rows[a][:, :, :].rearrange("p (c a) n -> p c (a n)", c=CH) for a in (1, 2)]

        def mask_number(att, batch):
            if att == 1:
                return 0 if isinstance(batch, int) and batch == 0 else 2 * batch - 1
            if isinstance(batch, int) and batch == B - 1:
                return 2 * B - 1
            return 2 * batch + 2

        def schedule(do_setup, do_project, do_half, do_drain, loop):
            do_setup()
            start = Half(1, 0, 0, 0, side=Side(1, 1, 1), ahead=False)
            do_half(start)
            do_half(Half(1, 1, 1, 1, before=start, ahead=False))
            do_project(Side(2, 0, 0))
            with loop(0, (B - 4) // 2) as i:
                for par in (0, 1):
                    do_half(second_half(2 * i + par, par))
                    do_half(first_half(2 * i + par + 2, par))
            do_half(second_half(B - 4, 0))
            do_half(first_half(B - 2, 0))
            do_half(second_half(B - 3, 1, ahead=False))
            do_half(first_half(B - 1, 1, ahead=False))
            end = second_half(B - 2, 0, side=False, ahead=False)
            do_half(end)
            do_project(Side(2, B - 1, 1))
            last = Half(2, B - 1, 1, 2 * B - 1, before=end, ahead=False)
            do_half(last)
            do_drain(last)

        block = ctx.enter_context(nc.Block())

        @block.sync
        def _(sp):
            def load_x(batch, par):
                hold(sp, s_passed["sp"])
                sp.dma_start(pe[par][:, :, :], x[bass.ds(batch * N, N), :].rearrange(
                    "(t p) d -> p t d", p=P)).then_inc(s_x, 16)

            def load_adj(att, batch):
                src = adj_t if att == 1 else adj
                hold(sp, s_passed["sp"])
                sp.dma_start(adj_raw[:, :, :], src[bass.ds(batch * N, N), :].rearrange(
                    "(t p) n -> p t n", p=P)).then_inc(s_adj, 16)

            def store_pe(batch, par):
                sp.wait_ge(s_pe, batch + 1)
                hold(sp, s_passed["sp"])
                sp.dma_start(peeled_rows[bass.ds(batch * N, N), :].rearrange(
                    "(t p) d -> p t d", p=P), pe[par][:, :, :]).then_inc(s_pe_stored, 16)

            def store_node(half):
                sp.wait_ge(s_ln, half.pos + 1)
                hold(sp, s_passed["sp"])
                for t in range(NT):
                    sp.dma_start(node_rows[bass.ds(half.batch * N + t * P, P), :].rearrange(
                        "p (c n) -> p c n", c=PAIRS), rows[half.slot][:, :, t * P:(t + 1) * P]).then_inc(s_node, 16)
                sp.wait_ge(s_node, (half.batch + 1) * 16 * NT)
                hold(sp, s_passed["sp"])

            def setup():
                load_x(0, 0)
                for n in COLUMN_VECTORS:
                    sp.dma_start(col[n][:, :], columns[n]).then_inc(s_columns, 16)
                for n in range(HALVES):
                    if n >= 2:
                        sp.wait_ge(s_w_hi, n - 1)
                        hold(sp, s_passed["sp"])
                        sp.wait_ge(s_w_lo, n - 1)
                        hold(sp, s_passed["sp"])
                    src = w[WEIGHTS[n // 2]].rearrange("(c p) o -> p c o", p=P)
                    sp.dma_start(stage[n % 2], src[:, CH * (n % 2):CH * (n % 2) + CH, :]).then_inc(s_stage[n % 2], 16)
                    if n == 5:
                        sp.wait_ge(s_x, 16)
                        load_x(1, 1)
                        load_adj(1, 0)
                        for a, src in ((1, bv1_row), (2, bv2_row)):
                            sp.dma_start(bv_row[a][:, :], src.to_broadcast([P, D])).then_inc(s_bv, 16)
                sp.wait_ge(s_mask, 1)
                load_adj(1, 1)
                store_pe(0, 0)
                store_pe(1, 1)

            def project(side):
                if side.batch == 0:
                    store_pe(2, 0)

            def half(h):
                if h.att == 2:
                    if not h.is_last:
                        sp.wait_ge(s_mask, mask_number(2, h.batch + 1))
                        hold(sp, s_passed["sp"])
                        load_adj(2, h.batch + 1)
                    sp.wait_ge(s_res, 2 * h.batch + 1)
                    hold(sp, s_passed["sp"])
                    sp.wait_ge(s_pe_stored, (h.batch + 1) * 16)
                    hold(sp, s_passed["sp"])
                    sp.dma_start(pe_again[:, :, :], peeled_rows[bass.ds(h.batch * N, N), :].rearrange(
                        "(t p) d -> p t d", p=P)).then_inc(s_pe_again, 16)
                    if h.ahead:
                        sp.wait_ge(s_res, h.before.pos + 1)
                        hold(sp, s_passed["sp"])
                        sp.wait_ge(s_pe_stored, (h.batch + 2) * 16)
                        hold(sp, s_passed["sp"])
                        sp.wait_ge(s_x, (h.batch + 3) * 16)
                        hold(sp, s_passed["sp"])
                        load_x(h.batch + 3, 1 - h.par)
                    if h.is_last:
                        store_node(h.before)
                elif h.is_first:
                    sp.wait_ge(s_mask, 2)
                    hold(sp, s_passed["sp"])
                    load_adj(2, 0)
                elif h.is_second:
                    sp.wait_ge(s_mask, 3)
                    hold(sp, s_passed["sp"])
                    load_adj(1, 2)
                    sp.wait_ge(s_res, 1)
                    hold(sp, s_passed["sp"])
                    sp.wait_ge(s_pe_stored, 32)
                    hold(sp, s_passed["sp"])
                    load_x(2, 0)
                else:
                    if h.ahead:
                        sp.wait_ge(s_mask, mask_number(1, h.batch + 1))
                        hold(sp, s_passed["sp"])
                        load_adj(1, h.batch + 1)
                        store_pe(h.batch + 1, 1 - h.par)
                    if h.before is not None:
                        store_node(h.before)

            def drain(h):
                store_node(h)

            schedule(setup, project, half, drain, sp.Fori)

        @block.gpsimd
        def _(pool):
            def build_mask(att, batch, head0):
                number = mask_number(att, batch)
                pool.wait_ge(s_adj, (number + 1) * 16)
                at_least(pool, s_max, head0)
                hold(pool, s_passed["pool"])
                pool.tensor_scalar(mask[slot_of(att, batch)][:, :, :], adj_raw[:, :, :], 0.0, MASKED, ALU.is_le, ALU.mult)\
                    .then_inc(s_mask, 1)

            def setup():
                pool.memset(ident[:, :], 0.0).then_inc(s_consts, 1)
                pool.wait_ge(s_consts, 1)
                pool.affine_select(out=ident[:, :], in_=ident[:, :], compare_op=ALU.not_equal, fill=1.0,
                                   base=0, pattern=[[-1, P]], channel_multiplier=1).then_inc(s_consts, 1)
                pool.memset(neg_half[:, :], -0.5).then_inc(s_consts, 1)
                pool.wait_ge(s_consts, 3)
                x_power(0)
                for a in (2, 1):
                    pool.memset(q_hi[a][:, :, :].bitcast(F32), 0.0).then_inc(s_zeros, 1)
                    pool.memset(q_lo[a][:, :, :].bitcast(F32), 0.0).then_inc(s_zeros, 1)
                build_mask(1, 0, 0)
                x_power(1)

            def x_power(batch):
                pool.wait_ge(s_x_var, batch + 1)
                pool.tensor_tensor(x_rstd[:, :], x_var[:, :], neg_half[:, :], ALU.pow).then_inc(s_x_rstd, 1)

            def residual(h):
                pool.wait_ge(s_rows, (h.pos + 1) * PAIRS)
                pool.wait_ge(s_inv, h.pos + 1)
                if h.att == 2:
                    pool.wait_ge(s_pe_again, (h.batch + 1) * 16)
                src = pe_again if h.att == 2 else pe[h.par]
                for t in range(NT):
                    r = rows[h.slot][:, :, t * P:(t + 1) * P]
                    heads = r.rearrange("p c (a d) -> p c a d", a=2)
                    inv = inv_sums[:, t, :].rearrange("p (c a) -> p c a", a=2).unsqueeze(3)\
                        .to_broadcast([P, PAIRS, 2, HD])
                    pool.tensor_tensor(heads, heads, inv, ALU.mult).then_inc(s_res_step, 1)
                for t in range(NT):
                    r = rows[h.slot][:, :, t * P:(t + 1) * P]
                    add = src[:, t, :].rearrange("p (c n) -> p c n", c=PAIRS)
                    pool.wait_ge(s_res_step, 4 * h.pos + t + 1)
                    pool.tensor_tensor(r, r, add, ALU.add).then_inc(s_res_step, 1)
                for t in range(NT):
                    r = rows[h.slot][:, :, t * P:(t + 1) * P]
                    bias = bv_row[h.att][:, :].rearrange("p (c n) -> p c n", c=PAIRS)
                    pool.wait_ge(s_res_step, 4 * h.pos + NT + t + 1)
                    add = pool.tensor_tensor(r, r, bias, ALU.add)
                add.then_inc(s_res, 1)

            def row_power(h):
                pool.wait_ge(s_row_var, h.pos + 1)
                pool.tensor_tensor(row_rstd[:, :], row_var[:, :], neg_half[:, :], ALU.pow).then_inc(s_row_rstd, 1)

            def project(side):
                if side.batch == 0:
                    x_power(2)
                else:
                    build_mask(2, B - 1, H * (2 * B - 2))

            def half(h):
                if h.is_first:
                    build_mask(1, 1, 0)
                elif h.is_second:
                    build_mask(2, 0, h.head0)
                elif h.side is not None:
                    if h.att == 2:
                        build_mask(1, h.batch + 2, h.head0)
                    else:
                        build_mask(2, h.batch - 1, h.head0)
                if h.att == 1 and h.ahead:
                    x_power(h.batch + 1)
                if h.before is not None:
                    residual(h.before)
                if h.before is not None:
                    row_power(h.before)

            def drain(h):
                residual(h)
                row_power(h)

            schedule(setup, project, half, drain, pool.Fori)

        @block.tensor
        def _(pe_eng):
            mm, tr = pe_eng.matmul, pe_eng.transpose

            def three(out, stat_hi, stat_lo, mov_hi, mov_lo, first, last):
                mm(out, stat_hi, mov_hi, start=first, stop=False)
                mm(out, stat_hi, mov_lo, start=False, stop=False)
                return mm(out, stat_lo, mov_hi, start=False, stop=last)

            def group_ready(side, j, m):
                at_least(pe_eng, s_hi, m - 1)
                at_least(pe_eng, s_lo, m - 1)
                if j == 0:
                    if side.att == 1:
                        pe_eng.wait_ge(s_pe, side.batch + 1)
                    elif isinstance(side.batch, int) and side.batch == 0:
                        pe_eng.wait_ge(s_ln, 1)
                    else:
                        pe_eng.wait_ge(s_ln, 2 * side.batch)
                if j == 2:
                    pe_eng.wait_ge(s_hi, side.first + 2)
                    pe_eng.wait_ge(s_lo, side.first + 2)

            def side_piece(side, j, c):
                m, bank = side.first + j, proj_ps[j % 2]
                if c == 0:
                    group_ready(side, j, m)
                last = None
                if j < 2:
                    chunk = 2 * j + c
                    for t in range(NT):
                        src = pe[side.par][:, t, chunk * P:(chunk + 1) * P] if side.att == 1 else \
                            rows[slot_of(1, side.batch)][:, chunk, t * P:(t + 1) * P]
                        last = tr(bank[:, c * N + t * P:c * N + (t + 1) * P], src, ident[:, :])
                elif j < 6:
                    names = ("n2e_q_w", "n2e_k_w") if side.att == 1 else ("e2n_q_w", "e2n_k_w")
                    name = names[j % 2]
                    edge = side.att == 2 and j % 2 == 1
                    hi, lo = (edge_t_hi, edge_t_lo) if edge else (pe_t_hi[side.par], pe_t_lo[side.par])
                    o = (2 * ((j - 2) // 2) + c) * P
                    for d in range(DC):
                        last = three(bank[:, c * N:(c + 1) * N], w_hi[name][:, d, o:o + P], w_lo[name][:, d, o:o + P],
                                     hi[:, d, :], lo[:, d, :], d == 0, d == DC - 1)
                else:
                    name = "n2e_v_w" if side.att == 1 else "e2n_v_w"
                    hi, lo = (edge_t_hi, edge_t_lo) if side.att == 2 else (pe_t_hi[side.par], pe_t_lo[side.par])
                    t = j - 6
                    for d in range(2 * c, 2 * c + 2):
                        last = three(bank[:, :], hi[:, d, t * P:(t + 1) * P], lo[:, d, t * P:(t + 1) * P],
                                     w_hi[name][:, d, :], w_lo[name][:, d, :], d == 0, d == DC - 1)
                if c == 1:
                    last.then_inc(s_group, 1)

            def scores(h, u):
                g = h.head0 + u
                if u == 0:
                    first = Side(h.att, h.batch, h.par).first
                    pe_eng.wait_ge(s_hi, first + 6)
                    pe_eng.wait_ge(s_lo, first + 6)
                at_least(pe_eng, s_exp, g - 1)
                for t in range(NT):
                    q = (slice(None), u, slice(t * P, (t + 1) * P))
                    last = three(scores_ps[u % 2][:, t * N:(t + 1) * N], q_hi[h.slot][q], q_lo[h.slot][q],
                                 k_hi[h.slot][:, u // 2, :], k_lo[h.slot][:, u // 2, :], True, True)
                last.then_inc(s_scores, 1)

            def transpose_probs(h, u):
                g = h.head0 + u
                pe_eng.wait_ge(s_exp, g + 1)
                for j in range(NT):
                    for t in range(NT):
                        last = tr(probs_t_ps[u % 2][:, j * N + t * P:j * N + (t + 1) * P],
                                  probs[:, t, j * P:(j + 1) * P], ident[:, :])
                last.then_inc(s_probs_t, 1)

            def weigh_values(h, u):
                g = h.head0 + u
                if u == 0:
                    first = Side(h.att, h.batch, h.par).first
                    pe_eng.wait_ge(s_hi, first + GROUPS)
                    pe_eng.wait_ge(s_lo, first + GROUPS)
                if u % 2 == 0:
                    at_least(pe_eng, s_heads_t, h.pos * PAIRS + u // 2)
                pe_eng.wait_ge(s_pt_hi, g + 1)
                pe_eng.wait_ge(s_pt_lo, g + 1)
                out = heads_ps[:, (u % 2) * N:(u % 2 + 1) * N]
                for j in range(NT):
                    mm(out, v_both[h.slot][:, j, u, :], probs_t_hi[:, j, :], start=j == 0, stop=False)
                    last = mm(out, v_both[h.slot][:, j, u, :], probs_t_lo[:, j, :], start=False, stop=j == NT - 1)
                last.then_inc(s_pv, 1)

            def transpose_heads(h, p):
                pair = h.pos * PAIRS + p
                pe_eng.wait_ge(s_heads_t, pair + 1)
                at_least(pe_eng, s_rows, pair)
                for t in range(NT):
                    for a in range(2):
                        o = (t * 2 + a) * P
                        last = tr(rows_ps[:, o:o + P], heads_t[:, a, t * P:(t + 1) * P], ident[:, :])
                last.then_inc(s_rows_ps, 1)

            def bias_product(n):
                pe_eng.wait_ge(s_stage[n % 2], 16 * (n // 2 + 1))
                raw = stage[n % 2]
                if n < HALVES - 2:
                    pe_eng.wait_ge(s_columns, 16 * len(COLUMN_VECTORS))
                    for o in range(DC):
                        for c in range(CH):
                            d = CH * (n % 2) + c
                            last = mm(scores_ps[n % 2][:, o:o + 1], raw[:, c, o * P:(o + 1) * P],
                                      col["norm1_b"][:, d:d + 1], start=c == 0, stop=c == CH - 1)
                else:
                    pe_eng.wait_ge(s_b_bcast, 1)
                    for c in range(CH):
                        d = CH * (n % 2) + c
                        last = mm(heads_ps[:, :], probs[:, :, :].rearrange("p t n -> p (t n)")[:, d * P:(d + 1) * P],
                                  raw[:, c, :], start=d == 0, stop=d == DC - 1)
                last.then_inc(s_w_bias, 1)

            def setup():
                pe_eng.wait_ge(s_consts, 2)
                side = Side(1, 0, 0)
                for what, n in SETUP_ORDER:
                    if what == "g":
                        if n in (2, 3, 6):
                            pe_eng.wait_ge(s_w_hi, {2: 2, 3: 4, 6: 6}[n])
                            pe_eng.wait_ge(s_w_lo, {2: 2, 3: 4, 6: 6}[n])
                        side_piece(side, n, 0)
                        side_piece(side, n, 1)
                    elif n >= HALVES - 4:
                        bias_product(n)
                pe_eng.wait_ge(s_w_hi, HALVES)
                pe_eng.wait_ge(s_w_lo, HALVES)
                pe_eng.wait_ge(s_biases, 2)

            def project(side):
                for j in range(GROUPS):
                    side_piece(side, j, 0)
                    side_piece(side, j, 1)

            def half(h):
                for u in range(H):
                    scores(h, u)
                    if u % 2 == 0 and u >= 4:
                        transpose_heads(h, u // 2 - 2)
                    elif u % 2 == 0 and h.before is not None:
                        transpose_heads(h.before, PAIRS - 2 + u // 2)
                    if h.side is not None:
                        for j, c in SIDE_PIECES[u][0]:
                            side_piece(h.side, j, c)
                    if u >= 2:
                        weigh_values(h, u - 2)
                    elif h.before is not None:
                        weigh_values(h.before, H - 2 + u)
                    if u:
                        transpose_probs(h, u - 1)
                    elif h.before is not None:
                        transpose_probs(h.before, H - 1)
                    if h.side is not None:
                        for j, c in SIDE_PIECES[u][1]:
                            side_piece(h.side, j, c)

            def drain(h):
                transpose_heads(h, PAIRS - 2)
                weigh_values(h, H - 2)
                transpose_probs(h, H - 1)
                weigh_values(h, H - 1)
                transpose_heads(h, PAIRS - 1)

            schedule(setup, project, half, drain, pe_eng.Fori)

        @block.scalar
        def _(act):
            def project_hi(side, j):
                m, bank = side.first + j, proj_ps[j % 2]
                act.wait_ge(s_group, m + 1)
                if j < 2:
                    dst = pe_t_hi[side.par] if side.att == 1 else edge_t_hi
                    act.activation(dst[:, 2 * j:2 * j + 2, :].rearrange("p c n -> p (c n)"), bank[:, :], ACT.Copy)\
                        .then_inc(s_hi, 1)
                elif j < 6:
                    pair0 = 2 * ((j - 2) // 2)
                    for c in range(2):
                        src, ch = bank[:, c * N:(c + 1) * N], pair0 + c
                        if j % 2:
                            bias = col["n2e_k_b" if side.att == 1 else "e2n_k_b"]
                            last = act.activation(k_hi[side.slot][:, ch, :], src, ACT.Identity, bias=bias[:, ch:ch + 1])
                        else:
                            bias = col["n2e_q_b" if side.att == 1 else "e2n_q_b"]
                            for a in range(2):
                                s = slice(a * HD, (a + 1) * HD)
                                last = act.activation(q_hi[side.slot][s, 2 * ch + a, :], src[s, :], ACT.Identity,
                                                      bias=bias[s, ch:ch + 1])
                    last.then_inc(s_hi, 1)
                else:
                    t = j - 6
                    act.activation(v_both[side.slot][:, t, :, 0:HD], bank[:, :].rearrange("p (h d) -> p h d", h=H),
                                   ACT.Copy).then_inc(s_hi, 1)

            def exps(h, u):
                g = h.head0 + u
                act.wait_ge(s_max, g + 1)
                at_least(act, s_probs_t, g)
                for t in range(NT):
                    last = act.activation(probs[:, t, :], scores_ps[u % 2][:, t * N:(t + 1) * N], ACT.Exp,
                                          bias=neg_max[:, u % 2, t:t + 1], scale=-1.0,
                                          accum_out=sums[h.slot][:, t, u:u + 1])
                last.then_inc(s_exp, 1)

            def probs_hi(h, u):
                g = h.head0 + u
                act.wait_ge(s_probs_t, g + 1)
                at_least(act, s_pv, g)
                act.activation(probs_t_hi[:, :, :].rearrange("p t n -> p (t n)"), probs_t_ps[u % 2][:, :], ACT.Copy)\
                    .then_inc(s_pt_hi, 1)

            def heads_out(h, p):
                pair = h.pos * PAIRS + p
                act.wait_ge(s_pv, h.head0 + 2 * p + 2)
                at_least(act, s_rows_ps, pair)
                act.activation(heads_t[:, :, :].rearrange("p a n -> p (a n)"), heads_ps[:, :], ACT.Copy)\
                    .then_inc(s_heads_t, 1)

            def x_relu(batch, par):
                act.wait_ge(s_x_shift, batch + 1)
                for t in range(NT):
                    last = act.activation(pe[par][:, t, :], pe[par][:, t, :], ACT.Relu,
                                          bias=x_shift[:, t:t + 1], scale=x_rstd[:, t:t + 1])
                last.then_inc(s_pe, 1)

            def weight_hi(n):
                name = WEIGHTS[n // 2]
                if n < HALVES - 4:
                    act.wait_ge(s_stage[n % 2], 16 * (n // 2 + 1))
                else:
                    act.wait_ge(s_w_scaled, n - (HALVES - 4) + 1)
                act.activation(w_hi[name][:, CH * (n % 2):CH * (n % 2) + CH, :], stage[n % 2], ACT.Copy)\
                    .then_inc(s_w_hi, 1)

            def setup():
                act.wait_ge(s_columns, 16 * len(COLUMN_VECTORS))
                for what, n in SETUP_ORDER:
                    if what == "w":
                        weight_hi(n)
                        if n == 0:
                            x_relu(0, 0)
                        elif n == 7:
                            x_relu(1, 1)
                    else:
                        if n == 2:
                            act.wait_ge(s_zeros, 4)
                        project_hi(Side(1, 0, 0), n)
                act.wait_ge(s_biases, 2)

            def project(side):
                for j in range(GROUPS):
                    project_hi(side, j)
                    if side.batch == 0 and j == 3:
                        x_relu(2, 0)

            def half(h):
                for u in range(H):
                    if h.side is not None:
                        for j in SIDE_SPLITS[u]:
                            project_hi(h.side, j)
                    if u >= 3 and u % 2:
                        heads_out(h, (u - 3) // 2)
                    elif u == 1 and h.before is not None:
                        heads_out(h.before, PAIRS - 1)
                    if u:
                        probs_hi(h, u - 1)
                    elif h.before is not None:
                        probs_hi(h.before, H - 1)
                    exps(h, u)
                    if u == 3 and h.att == 1 and h.ahead:
                        x_relu(h.batch + 1, 1 - h.par)

            def drain(h):
                probs_hi(h, H - 1)
                heads_out(h, PAIRS - 1)

            schedule(setup, project, half, drain, act.Fori)

        @block.vector
        def _(dve):
            def project_lo(side, j):
                m, bank = side.first + j, proj_ps[j % 2]
                dve.wait_ge(s_hi, m + 1)
                if j < 2:
                    hi, lo = (pe_t_hi[side.par], pe_t_lo[side.par]) if side.att == 1 else (edge_t_hi, edge_t_lo)
                    s = (slice(None), slice(2 * j, 2 * j + 2), slice(None))
                    dve.tensor_tensor(lo[s].rearrange("p c n -> p (c n)"), bank[:, :],
                                      hi[s].rearrange("p c n -> p (c n)").bitcast(F32), ALU.subtract).then_inc(s_lo, 1)
                elif j < 6:
                    pair0 = 2 * ((j - 2) // 2)
                    for c in range(2):
                        src, ch = bank[:, c * N:(c + 1) * N], pair0 + c
                        if j % 2:
                            bias = col["n2e_k_b" if side.att == 1 else "e2n_k_b"]
                            last = dve.scalar_tensor_tensor(k_lo[side.slot][:, ch, :], src, bias[:, ch:ch + 1],
                                                            k_hi[side.slot][:, ch, :].bitcast(F32), ALU.add, ALU.subtract)
                        else:
                            bias = col["n2e_q_b" if side.att == 1 else "e2n_q_b"]
                            for a in range(2):
                                s = slice(a * HD, (a + 1) * HD)
                                last = dve.scalar_tensor_tensor(
                                    q_lo[side.slot][s, 2 * ch + a, :], src[s, :], bias[s, ch:ch + 1],
                                    q_hi[side.slot][s, 2 * ch + a, :].bitcast(F32), ALU.add, ALU.subtract)
                    last.then_inc(s_lo, 1)
                else:
                    t = j - 6
                    v = v_both[side.slot]
                    dve.tensor_tensor(v[:, t, :, HD:P], bank[:, :].rearrange("p (h d) -> p h d", h=H),
                                      v[:, t, :, 0:HD].bitcast(F32), ALU.subtract).then_inc(s_lo, 1)

            def maxima(h, u):
                g = h.head0 + u
                if u == 0:
                    dve.wait_ge(s_mask, mask_number(h.att, h.batch) + 1)
                dve.wait_ge(s_scores, g + 1)
                hold(dve, s_passed["dve"])
                for t in range(NT):
                    s = scores_ps[u % 2][:, t * N:(t + 1) * N]
                    last = dve.tensor_tensor_reduce(s, s, mask[h.slot][:, t, :], -SCALE, 3e38, ALU.add, ALU.min,
                                                    neg_max[:, u % 2, t:t + 1])
                last.then_inc(s_max, 1)

            def probs_lo(h, u):
                g = h.head0 + u
                dve.wait_ge(s_pt_hi, g + 1)
                dve.tensor_tensor(probs_t_lo[:, :, :].rearrange("p t n -> p (t n)"), probs_t_ps[u % 2][:, :],
                                  probs_t_hi[:, :, :].rearrange("p t n -> p (t n)").bitcast(F32), ALU.subtract)\
                    .then_inc(s_pt_lo, 1)

            def head_rows(h, p):
                pair = h.pos * PAIRS + p
                if p == 0 and h.att == 2 and not h.is_last:
                    dve.wait_ge(s_pe_again, (h.batch + 1) * 16)
                dve.wait_ge(s_rows_ps, pair + 1)
                dve.tensor_reduce(rows[h.slot][:, p, :].rearrange("p (a d) -> p a d", a=4),
                                  rows_ps[:, :].rearrange("p (a x d) -> p a d x", a=4, x=2), AX_X, ALU.add)\
                    .then_inc(s_rows, 1)

            def inverse_sums(h):
                dve.wait_ge(s_exp, h.head0 + H)
                dve.reciprocal(inv_sums[:, :, :].rearrange("p t h -> p (t h)"),
                               sums[h.slot][:, :, :].rearrange("p t h -> p (t h)")).then_inc(s_inv, 1)

            def moments(src, stats, mv, var, s_stats, s_var, count):
                for t in range(NT):
                    dve.bn_stats(stats[:, t, :], src(t)).then_inc(s_stats, 1)
                for t in range(NT):
                    dve.wait_ge(s_stats, count * 2 * NT + t + 1)
                    hold(dve, s_passed["dve"])
                    dve.bn_aggr(mv[:, t, :], stats[:, t, :]).then_inc(s_stats, 1)
                dve.wait_ge(s_stats, count * 2 * NT + 2 * NT)
                dve.tensor_scalar(var[:, :], mv[:, :, 1], LN_EPS, None, ALU.add).then_inc(s_var, 1)

            def x_moments(batch, par):
                dve.wait_ge(s_x, (batch + 1) * 16)
                moments(lambda t: pe[par][:, t, :], x_stats, x_mv, x_var, s_x_stats, s_x_var, batch)

            def x_shifts(batch):
                dve.wait_ge(s_x_rstd, batch + 1)
                dve.scalar_tensor_tensor(x_shift[:, :], x_mv[:, :, 0], -1.0, x_rstd[:, :], ALU.mult, ALU.mult)\
                    .then_inc(s_x_shift, 1)

            def row_moments(h):
                dve.wait_ge(s_res, h.pos + 1)
                moments(lambda t: rows[h.slot][:, :, t * P:(t + 1) * P], row_stats, row_mv, row_var,
                        s_row_stats, s_row_var, h.pos)

            def normalise(h):
                dve.wait_ge(s_row_rstd, h.pos + 1)
                for t in range(NT):
                    r = rows[h.slot][:, :, t * P:(t + 1) * P]
                    last = dve.tensor_scalar(r, r, row_mv[:, t, 0:1], row_rstd[:, t:t + 1], ALU.subtract, ALU.mult)
                last.then_inc(s_ln, 1)

            def weight_lo(n):
                name = WEIGHTS[n // 2]
                if n >= HALVES - 4:
                    k = n - (HALVES - 4)
                    dve.wait_ge(s_stage[n % 2], 16 * (n // 2 + 1))
                    dve.wait_ge(s_w_bias, k + 1)
                    for c in range(CH):
                        d = CH * (n % 2) + c
                        last = dve.tensor_scalar(stage[n % 2][:, c, :], stage[n % 2][:, c, :],
                                                 col["norm1_g"][:, d:d + 1], None, ALU.mult)
                    last.then_inc(s_w_scaled, 1)
                dve.wait_ge(s_w_hi, n + 1)
                s = (slice(None), slice(CH * (n % 2), CH * (n % 2) + CH), slice(None))
                dve.tensor_tensor(w_lo[name][s], stage[n % 2], w_hi[name][s].bitcast(F32), ALU.subtract)\
                    .then_inc(s_w_lo, 1)

            def setup():
                dve.wait_ge(s_columns, 16 * len(COLUMN_VECTORS))
                x_moments(0, 0)
                x_shifts(0)
                for c in range(DC):
                    last = dve.tensor_copy(probs[:, :, :].rearrange("p t n -> p (t n)")[:, c * P:(c + 1) * P],
                                           col["norm1_b"][:, c:c + 1].to_broadcast([P, P]))
                last.then_inc(s_b_bcast, 1)
                for what, n in SETUP_ORDER:
                    if what == "w":
                        weight_lo(n)
                        if n == 6:
                            dve.wait_ge(s_pe, 1)
                            x_moments(1, 1)
                            x_shifts(1)
                    else:
                        project_lo(Side(1, 0, 0), n)
                dve.tensor_copy(bias_parts[:, 0:DC], scores_ps[0][:, 0:DC]).then_inc(s_biases, 1)
                dve.wait_ge(s_biases, 1)
                dve.tensor_tensor(bias_parts[:, DC:2 * DC], scores_ps[1][:, 0:DC], bias_parts[:, 0:DC], ALU.add)\
                    .then_inc(s_b_bcast, 1)
                dve.wait_ge(s_b_bcast, 2)
                dve.tensor_tensor(col["e2n_k_b"][:, :], col["e2n_k_b"][:, :], bias_parts[:, DC:2 * DC], ALU.add)\
                    .then_inc(s_b_bcast, 1)
                dve.wait_ge(s_bv, 32)
                dve.tensor_tensor(bv_row[2][:, :], heads_ps[:, :], bv_row[2][:, :], ALU.add).then_inc(s_b_bcast, 1)
                dve.wait_ge(s_b_bcast, 4)
                dve.tensor_copy(bias_parts[:, 0:1], neg_half[:, 0:1]).then_inc(s_biases, 1)

            def project(side):
                for j in range(GROUPS):
                    project_lo(side, j)
                    if side.batch == 0 and j == 1:
                        x_moments(2, 0)
                    if side.batch == 0 and j == 2:
                        x_shifts(2)

            def half(h):
                for u in range(H):
                    maxima(h, u)
                    if h.side is not None:
                        for j in SIDE_SPLITS[u]:
                            project_lo(h.side, j)
                    if u % 2 == 0 and u >= 4:
                        head_rows(h, u // 2 - 2)
                    elif u % 2 == 0 and h.before is not None:
                        head_rows(h.before, PAIRS - 2 + u // 2)
                    if u:
                        probs_lo(h, u - 1)
                    elif h.before is not None:
                        probs_lo(h.before, H - 1)
                    if h.att == 1 and h.ahead:
                        if u == 1:
                            x_moments(h.batch + 1, 1 - h.par)
                        if u == 2:
                            x_shifts(h.batch + 1)
                    if h.before is not None:
                        if u == 1:
                            inverse_sums(h.before)
                        if u == 5:
                            row_moments(h.before)
                        if u == 6:
                            normalise(h.before)

            def drain(h):
                head_rows(h, PAIRS - 2)
                probs_lo(h, H - 1)
                inverse_sums(h)
                head_rows(h, PAIRS - 1)
                row_moments(h)
                normalise(h)

            schedule(setup, project, half, drain, dve.Fori)


def feed_forward_part(nc, x, node_rows, w1, w2, gain2_col, bias2_col, b1_col, row_vectors, out):
    with ExitStack() as ctx:
        def sb(name, shape, dt=F32):
            return ctx.enter_context(nc.sbuf_tensor(name, shape, dt))

        def ps(name):
            return ctx.enter_context(nc.psum_tensor(name, [P, 512], F32))

        def sem(name):
            return ctx.enter_context(nc.semaphore(name))

        w1_hi, w1_lo = sb("w1_hi", [P, DC, FF], F32R), sb("w1_lo", [P, DC, FF], F32R)
        w2_hi, w2_lo = sb("w2_hi", [P, FT, D], F32R), sb("w2_lo", [P, FT, D], F32R)
        z = [sb(f"z{i}", [P, RT, D]) for i in range(2)]
        xr = [sb(f"xr{i}", [P, RT, D]) for i in range(2)]
        z_t_hi, z_t_lo = sb("z_t_hi", [P, DC, ROWS], F32R), sb("z_t_lo", [P, DC, ROWS], F32R)
        hid = [sb(f"hid{i}", [P, ROWS]) for i in range(2)]
        hid_hi = [sb(f"hid_hi{i}", [P, ROWS], F32R) for i in range(2)]
        hid_lo = [sb(f"hid_lo{i}", [P, ROWS], F32R) for i in range(2)]
        gain2, bias2, gain3, bias3, b2_row = (sb(n, [P, D]) for n in ("gain2", "bias2", "gain3", "bias3", "b2_row"))
        gain2_c, bias2_c, b1_c = sb("gain2_c", [P, DC]), sb("bias2_c", [P, DC]), sb("b1_c", [P, FT])
        ident2 = sb("ident2", [P, P])
        neg_half2 = sb("neg_half2", [P, RT])
        stats, mv = sb("stats", [P, RT, BN_S]), sb("mv", [P, RT, BN_A])
        var, rstd = sb("var", [P, RT]), sb("rstd", [P, RT])

        hid_ps = [ps(f"hid_ps{i}") for i in range(2)]
        t_ps = [ps(f"t_ps{i}") for i in range(2)]
        out_ps = [ps(f"out_ps{i}") for i in range(RT)]

        f_passed = {e: sem(f"ff_passed_{e}") for e in ("sp", "dve")}
        f_vec = sem("ff_vectors_loaded")
        f_const = sem("ff_constants")
        f_stage = [sem(f"ff_staged{i}") for i in range(2)]
        f_w_scaled = sem("ff_scaled")
        f_w_hi = sem("ff_weights_hi")
        f_w_lo = sem("ff_weights_lo")
        f_w_bias = sem("ff_bias_products")
        f_b1 = sem("ff_b1_ready")
        f_b2 = sem("ff_b2_ready")
        f_z = [sem(f"z_loaded{i}") for i in range(2)]
        f_x = [sem(f"x_again_loaded{i}") for i in range(2)]
        f_t = sem("z_transposed")
        f_t_hi = sem("z_t_hi_ready")
        f_t_lo = sem("z_t_lo_ready")
        f_hid_ps = sem("hid_done")
        f_hid = sem("gelu_ready")
        f_hid_hi = sem("hid_hi_ready")
        f_hid_lo = sem("hid_lo_ready")
        f_hid_used = sem("hid_used")
        f_node_step = sem("node_step")
        f_node = sem("node_features_ready")
        f_x_bias = sem("x_biased")
        f_out_ps = sem("out_done")
        f_sum = sem("sum_ready")
        f_stats = sem("ff_stats")
        f_var = sem("ff_var")
        f_rstd = sem("ff_rstd")
        f_norm = sem("ff_normalised")
        f_gain = sem("ff_gain")
        f_final = sem("ff_final")
        f_stored = [sem(f"out_stored{i}") for i in range(2)]

        STAGES = 2 * DC

        def stage_of(n):
            return z[n % 2][:, :, :].rearrange("p t d -> p (t d)")

        def weight_part(n, one, two):
            if n < DC:
                return one[:, n, :]
            q = FT // DC
            return two[:, (n - DC) * q:(n - DC + 1) * q, :].rearrange("p f d -> p (f d)")

        def schedule(do_setup, do_pass, loop):
            do_setup()
            do_pass(0, 0, 0)
            do_pass(1, 1, 0)
            with loop(1, PASSES // 2 - 1) as i:
                do_pass(2 * i, 0, i)
                do_pass(2 * i + 1, 1, i)
            do_pass(PASSES - 2, 0, PASSES // 2 - 1)
            do_pass(PASSES - 1, 1, PASSES // 2 - 1, last=True)

        block = ctx.enter_context(nc.Block())

        @block.sync
        def _(sp):
            def load(dst, src, r, s):
                hold(sp, f_passed["sp"])
                sp.dma_start(dst[:, :, :], src[bass.ds(r * ROWS, ROWS), :].rearrange(
                    "(t p) d -> p t d", p=P)).then_inc(s, 16)

            def setup():
                for dst, src in ((gain2_c, gain2_col), (bias2_c, bias2_col), (b1_c, b1_col)):
                    sp.dma_start(dst[:, :], src).then_inc(f_vec, 16)
                for dst, src in zip((gain2, bias2, gain3, bias3, b2_row), row_vectors):
                    sp.dma_start(dst[:, :], src.to_broadcast([P, D])).then_inc(f_vec, 16)
                for n in range(STAGES):
                    if n >= 2:
                        sp.wait_ge(f_w_hi, n - 1)
                        hold(sp, f_passed["sp"])
                        sp.wait_ge(f_w_lo, n - 1)
                        hold(sp, f_passed["sp"])
                    src = w1[n * P:(n + 1) * P, :] if n < DC else \
                        w2[(n - DC) * D:(n - DC + 1) * D, :].rearrange("(f p) d -> p f d", p=P)
                    dst = z[n % 2][:, :, :].rearrange("p t d -> p (t d)") if n < DC else z[n % 2][:, :, :]
                    sp.dma_start(dst, src).then_inc(f_stage[n % 2], 16)
                sp.wait_ge(f_w_hi, STAGES)
                hold(sp, f_passed["sp"])
                sp.wait_ge(f_w_lo, STAGES)
                hold(sp, f_passed["sp"])
                load(z[0], node_rows, 0, f_z[0])
                load(xr[0], x, 0, f_x[0])

            def do_pass(r, par, i, last=False):
                if not last:
                    nxt = 1 - par
                    if not (isinstance(r, int) and r == 0):
                        sp.wait_ge(f_final, r * RT)
                        hold(sp, f_passed["sp"])
                        sp.wait_ge(f_stored[nxt], (i + par) * RT * 16)
                        hold(sp, f_passed["sp"])
                    load(z[nxt], node_rows, r + 1, f_z[nxt])
                    load(xr[nxt], x, r + 1, f_x[nxt])
                for t in range(RT):
                    sp.wait_ge(f_final, r * RT + t + 1)
                    hold(sp, f_passed["sp"])
                    sp.dma_start(out[bass.ds(r * ROWS + t * P, P), :], xr[par][:, t, :]).then_inc(f_stored[par], 16)
                if isinstance(r, int) and r >= PASSES - 2:
                    sp.wait_ge(f_stored[par], (i + 1) * RT * 16)
                    hold(sp, f_passed["sp"])

            schedule(setup, do_pass, sp.Fori)

        @block.gpsimd
        def _(pool):
            def setup():
                pool.memset(ident2[:, :], 0.0).then_inc(f_const, 1)
                pool.wait_ge(f_const, 1)
                pool.affine_select(out=ident2[:, :], in_=ident2[:, :], compare_op=ALU.not_equal, fill=1.0,
                                   base=0, pattern=[[-1, P]], channel_multiplier=1).then_inc(f_const, 1)
                pool.memset(neg_half2[:, :], -0.5).then_inc(f_const, 1)
                pool.wait_ge(f_vec, 16 * 8)
                pool.tensor_tensor(bias2[:, :], bias2[:, :], b2_row[:, :], ALU.add).then_inc(f_b2, 1)
                pool.wait_ge(f_b2, 1)
                pool.wait_ge(f_const, 3)

            def finish(r, par):
                for t in range(RT):
                    pool.wait_ge(f_norm, r * RT + t + 1)
                    pool.tensor_tensor(z[par][:, t, :], z[par][:, t, :], gain3[:, :], ALU.mult).then_inc(f_gain, 1)
                for t in range(RT):
                    pool.wait_ge(f_gain, r * RT + t + 1)
                    pool.tensor_tensor(xr[par][:, t, :], xr[par][:, t, :], z[par][:, t, :], ALU.add)\
                        .then_inc(f_final, 1)

            def power(r):
                pool.wait_ge(f_var, r + 1)
                pool.tensor_tensor(rstd[:, :], var[:, :], neg_half2[:, :], ALU.pow).then_inc(f_rstd, 1)

            def do_pass(r, par, i, last=False):
                if not (isinstance(r, int) and r == 0):
                    power(r - 1)
                    finish(r - 1, 1 - par)
                pool.wait_ge(f_x[par], (i + 1) * 16)
                for t in range(RT):
                    pool.tensor_tensor(xr[par][:, t, :], xr[par][:, t, :], bias3[:, :], ALU.add).then_inc(f_x_bias, 1)
                pool.wait_ge(f_z[par], (i + 1) * 16)
                pool.wait_ge(f_t, r * DC + DC)
                for t in range(RT):
                    pool.tensor_tensor(z[par][:, t, :], z[par][:, t, :], gain2[:, :], ALU.mult).then_inc(f_node_step, 1)
                for t in range(RT):
                    pool.wait_ge(f_node_step, r * RT + t + 1)
                    pool.tensor_tensor(z[par][:, t, :], z[par][:, t, :], bias2[:, :], ALU.add).then_inc(f_node, 1)
                pool.wait_ge(f_x_bias, (r + 1) * RT)
                if last:
                    power(r)
                    finish(r, par)

            schedule(setup, do_pass, pool.Fori)

        @block.tensor
        def _(pe_eng):
            mm, tr = pe_eng.matmul, pe_eng.transpose

            def transpose_rows(r, par, i, c):
                if c == 0:
                    pe_eng.wait_ge(f_z[par], (i + 1) * 16)
                if not (isinstance(r, int) and r == 0 and c < 2):
                    pe_eng.wait_ge(f_t_hi, r * DC + c - 1)
                    pe_eng.wait_ge(f_t_lo, r * DC + c - 1)
                for t in range(RT):
                    last = tr(t_ps[c % 2][:, t * P:(t + 1) * P], z[par][:, t, c * P:(c + 1) * P], ident2[:, :])
                last.then_inc(f_t, 1)

            def hidden(r, f):
                n = r * FT + f
                if f == 0:
                    pe_eng.wait_ge(f_t_hi, (r + 1) * DC)
                    pe_eng.wait_ge(f_t_lo, (r + 1) * DC)
                if not (isinstance(r, int) and r == 0 and f < 2):
                    pe_eng.wait_ge(f_hid, n - 1)
                o = hid_ps[f % 2][:, :]
                s = slice(f * P, (f + 1) * P)
                for d in range(DC):
                    mm(o, w1_hi[:, d, s], z_t_hi[:, d, :], start=d == 0, stop=False)
                    mm(o, w1_hi[:, d, s], z_t_lo[:, d, :], start=False, stop=False)
                    last = mm(o, w1_lo[:, d, s], z_t_hi[:, d, :], start=False, stop=d == DC - 1)
                last.then_inc(f_hid_ps, 1)

            def outcome(r, f):
                n = r * FT + f
                pe_eng.wait_ge(f_hid_hi, n + 1)
                pe_eng.wait_ge(f_hid_lo, n + 1)
                for t in range(RT):
                    if f == 0 and not (isinstance(r, int) and r == 0):
                        pe_eng.wait_ge(f_sum, (r - 1) * RT + t + 1)
                    s = slice(t * P, (t + 1) * P)
                    o = out_ps[t][:, :]
                    mm(o, hid_hi[f % 2][:, s], w2_hi[:, f, :], start=f == 0, stop=False)
                    mm(o, hid_hi[f % 2][:, s], w2_lo[:, f, :], start=False, stop=False)
                    last = mm(o, hid_lo[f % 2][:, s], w2_hi[:, f, :], start=False, stop=f == FT - 1)
                    if f == FT - 1:
                        last.then_inc(f_out_ps, 1)
                        last = None
                if last is not None:
                    last.then_inc(f_hid_used, 1)

            def setup():
                pe_eng.wait_ge(f_vec, 16 * 8)
                for n in range(DC):
                    pe_eng.wait_ge(f_stage[n % 2], 16 * (n // 2 + 1))
                    for f in range(FT):
                        last = mm(hid_ps[0][:, n * FT + f:n * FT + f + 1], stage_of(n)[:, f * P:(f + 1) * P],
                                  bias2_c[:, n:n + 1], start=True, stop=True)
                    last.then_inc(f_w_bias, 1)
                pe_eng.wait_ge(f_const, 2)
                pe_eng.wait_ge(f_w_hi, STAGES)
                pe_eng.wait_ge(f_w_lo, STAGES)
                pe_eng.wait_ge(f_b1, 4)
                for c in range(DC):
                    transpose_rows(0, 0, 0, c)

            def do_pass(r, par, i, last=False):
                for f in range(FT):
                    hidden(r, f)
                    if f == FT - 1 and not last:
                        transpose_rows(r + 1, 1 - par, i + par, 0)
                        transpose_rows(r + 1, 1 - par, i + par, 1)
                    if f:
                        outcome(r, f - 1)
                if not last:
                    transpose_rows(r + 1, 1 - par, i + par, 2)
                    transpose_rows(r + 1, 1 - par, i + par, 3)
                outcome(r, FT - 1)

            schedule(setup, do_pass, pe_eng.Fori)

        @block.scalar
        def _(act):
            def rows_hi(r, c):
                act.wait_ge(f_t, r * DC + c + 1)
                act.activation(z_t_hi[:, c, :], t_ps[c % 2][:, :], ACT.Copy).then_inc(f_t_hi, 1)

            def setup():
                for n in range(STAGES):
                    if n < DC:
                        act.wait_ge(f_w_scaled, n + 1)
                    else:
                        act.wait_ge(f_stage[n % 2], 16 * (n // 2 + 1))
                    act.activation(weight_part(n, w1_hi, w2_hi), stage_of(n), ACT.Copy).then_inc(f_w_hi, 1)
                act.wait_ge(f_b1, 4)
                for c in range(DC):
                    rows_hi(0, c)

            def do_pass(r, par, i, last=False):
                for f in range(FT):
                    n = r * FT + f
                    act.wait_ge(f_hid_ps, n + 1)
                    if not (isinstance(r, int) and r == 0 and f < 2):
                        act.wait_ge(f_hid_lo, n - 1)
                    act.activation(hid[f % 2][:, :], hid_ps[f % 2][:, :], ACT.Gelu, bias=b1_c[:, f:f + 1])\
                        .then_inc(f_hid, 1)
                if not last:
                    for c in range(DC):
                        rows_hi(r + 1, c)

            schedule(setup, do_pass, act.Fori)

        @block.vector
        def _(dve):
            def rows_lo(r, c):
                dve.wait_ge(f_t_hi, r * DC + c + 1)
                dve.tensor_tensor(z_t_lo[:, c, :], t_ps[c % 2][:, :], z_t_hi[:, c, :].bitcast(F32), ALU.subtract)\
                    .then_inc(f_t_lo, 1)

            def setup():
                dve.wait_ge(f_vec, 16 * 8)
                for n in range(STAGES):
                    if n < DC:
                        dve.wait_ge(f_stage[n % 2], 16 * (n // 2 + 1))
                        dve.wait_ge(f_w_bias, n + 1)
                        dve.tensor_scalar(stage_of(n), stage_of(n), gain2_c[:, n:n + 1], None, ALU.mult)\
                            .then_inc(f_w_scaled, 1)
                    dve.wait_ge(f_w_hi, n + 1)
                    dve.tensor_tensor(weight_part(n, w1_lo, w2_lo), stage_of(n),
                                      weight_part(n, w1_hi, w2_hi).bitcast(F32), ALU.subtract).then_inc(f_w_lo, 1)
                for n in range(DC):
                    if n:
                        dve.wait_ge(f_b1, n)
                    dve.tensor_tensor(b1_c[:, :], hid_ps[0][:, n * FT:(n + 1) * FT], b1_c[:, :], ALU.add)\
                        .then_inc(f_b1, 1)
                for c in range(DC):
                    rows_lo(0, c)

            def split(r, f):
                n = r * FT + f
                dve.wait_ge(f_hid, n + 1)
                if not (isinstance(r, int) and r == 0 and f < 2):
                    if f >= 2:
                        dve.wait_ge(f_hid_used, r * (FT - 1) + f - 1)
                    elif f == 1:
                        dve.wait_ge(f_out_ps, r * RT)
                    else:
                        dve.wait_ge(f_hid_used, r * (FT - 1))
                dve.tensor_copy(hid_hi[f % 2][:, :], hid[f % 2][:, :]).then_inc(f_hid_hi, 1)
                dve.wait_ge(f_hid_hi, n + 1)
                dve.tensor_tensor(hid_lo[f % 2][:, :], hid[f % 2][:, :], hid_hi[f % 2][:, :].bitcast(F32), ALU.subtract)\
                    .then_inc(f_hid_lo, 1)

            def moments(r, par):
                for t in range(RT):
                    dve.wait_ge(f_sum, r * RT + t + 1)
                    dve.bn_stats(stats[:, t, :], z[par][:, t, :]).then_inc(f_stats, 1)

            def spread(r):
                for t in range(RT):
                    dve.wait_ge(f_stats, r * 2 * RT + t + 1)
                    hold(dve, f_passed["dve"])
                    dve.bn_aggr(mv[:, t, :], stats[:, t, :]).then_inc(f_stats, 1)
                dve.wait_ge(f_stats, (r + 1) * 2 * RT)
                dve.tensor_scalar(var[:, :], mv[:, :, 1], LN_EPS, None, ALU.add).then_inc(f_var, 1)

            def normalise(r, par):
                dve.wait_ge(f_rstd, r + 1)
                for t in range(RT):
                    dve.tensor_scalar(z[par][:, t, :], z[par][:, t, :], mv[:, t, 0:1], rstd[:, t:t + 1],
                                      ALU.subtract, ALU.mult).then_inc(f_norm, 1)

            def sums(r, par):
                for t in range(RT):
                    dve.wait_ge(f_out_ps, r * RT + t + 1)
                    dve.wait_ge(f_node, r * RT + t + 1)
                    dve.tensor_tensor(z[par][:, t, :], out_ps[t][:, :], z[par][:, t, :], ALU.add).then_inc(f_sum, 1)

            def do_pass(r, par, i, last=False):
                for f in range(FT):
                    split(r, f)
                    if not (isinstance(r, int) and r == 0):
                        if f == 1:
                            moments(r - 1, 1 - par)
                            spread(r - 1)
                        if f == 3:
                            normalise(r - 1, 1 - par)
                if not last:
                    for c in range(DC):
                        rows_lo(r + 1, c)
                sums(r, par)
                if last:
                    moments(r, par)
                    spread(r)
                    normalise(r, par)

            schedule(setup, do_pass, dve.Fori)


def kernel(**inputs):
    import numpy as np
    import concourse.bacc as bacc
    from concourse.bass_utils import run_bass_kernel_spmd

    nc = bacc.Bacc("TRN2", target_bir_lowering=False, num_devices=1, dynamic_dma_scratch_size=1024)
    arrays = {}

    def given(name, a):
        a = np.ascontiguousarray(a)
        arrays[name] = a
        return nc.dram_tensor(name, a.shape, mybir.dt.from_np(a.dtype), kind="ExternalInput").ap()

    def vector(name):
        return np.asarray(inputs["L0_gnn_" + name])

    def column(name):
        return vector(name).reshape(-1, P).T

    def row(name):
        return given(name + "_row", vector(name).reshape(1, -1))

    x = given("x", np.asarray(inputs["x"]).reshape(B * N, D))
    a = np.asarray(inputs["adj"])
    adj = given("adj", a.reshape(B * N, N))
    adj_t = given("adj_t", a.transpose(0, 2, 1).reshape(B * N, N))
    w = {n: given(n, vector(n).T) for n in WEIGHTS}
    columns = {n: given(n + "_c", column(n)) for n in COLUMN_VECTORS}
    bv1, bv2 = row("n2e_v_b"), row("e2n_v_b")
    w1, w2 = given("ffn_w1", vector("ffn_w1").T), given("ffn_w2", vector("ffn_w2").T)
    gain2_c, bias2_c = given("gain2_in", column("norm2_g")), given("bias2_in", column("norm2_b"))
    b1_c = given("b1_in", column("ffn_b1"))
    row_vectors = [row(n) for n in ("norm2_g", "norm2_b", "norm3_g", "norm3_b", "ffn_b2")]
    pe_rows = nc.dram_tensor("pe_rows", [B * N, D], F32).ap()
    node_rows = nc.dram_tensor("node_rows", [B * N, D], F32).ap()
    out = nc.dram_tensor("out", [B * N, D], F32, kind="ExternalOutput").ap()
    attention_part(nc, x, adj, adj_t, w, columns, bv1, bv2, pe_rows, node_rows)
    feed_forward_part(nc, x, node_rows, w1, w2, gain2_c, bias2_c, b1_c, row_vectors, out)
    r = run_bass_kernel_spmd(nc, [arrays], core_ids=[0])
    return r.results[0]["out"].reshape(B, N, D)
```

```python
from contextlib import ExitStack

import concourse.bass as bass
from concourse import mybir

F32 = mybir.dt.float32
F32R = mybir.dt.float32r
BF16 = mybir.dt.bfloat16
ALU = mybir.AluOpType
ACT = mybir.ActivationFunctionType
AX_X = mybir.AxisListType.X

P = 128
B, N, D, H = 32, 256, 512, 8
HD = D // H
FF = 4 * D
DC = D // P
NT = N // P
PAIRS = H // 2
FT = FF // P
ROWS = 4 * P
RT = ROWS // P
PASSES = B * N // ROWS
SCALE = HD ** -0.5
LN_EPS = 1e-5
MASKED = -1e30
GROUPS = 8
BN_S, BN_A = 6, 2

SIDE_PIECES = [
    ([(0, 0), (0, 1), (1, 0), (1, 1)], []),
    ([(2, 0)], [(2, 1)]),
    ([(3, 0)], [(3, 1)]),
    ([(4, 0)], [(4, 1)]),
    ([(5, 0)], [(5, 1)]),
    ([(6, 0)], [(6, 1)]),
    ([(7, 0)], []),
    ([(7, 1)], []),
]
SIDE_SPLITS = [[0, 1], [], [2], [3], [4], [5], [6], [7]]

SETUP_ORDER = [("w", 0), ("w", 1), ("g", 0), ("g", 1), ("w", 2), ("w", 3), ("g", 2), ("w", 4), ("g", 3), ("w", 5),
               ("g", 4), ("w", 6), ("g", 5), ("w", 7), ("g", 6), ("w", 8), ("g", 7), ("w", 9), ("w", 10), ("w", 11)]

COLUMN_VECTORS = ["n2e_q_b", "n2e_k_b", "e2n_q_b", "e2n_k_b", "norm1_g", "norm1_b"]
WEIGHTS = ["n2e_q_w", "n2e_k_w", "n2e_v_w", "e2n_q_w", "e2n_k_w", "e2n_v_w"]


def hold(engine, passed):
    engine.sem_inc(passed, 1)


class FeedWeights:
    PARTS = 8
    HALVES = 2 * PARTS
    SIZE = FF
    AT_HEADS_BEFORE = {6: 0, 7: 1}
    AT_GROUPS = {1: 2, 3: 3, 5: 4, 7: 5}
    AT_HEADS_LAST = {u: 6 + u for u in range(H)}
    AT_END = (14, 15)

    def __init__(self, nc, ctx, w1, w2):
        self.region = ctx.enter_context(nc.sbuf_tensor("matrices", [P, 2 * self.PARTS * self.SIZE], F32R))
        self.w1_dram, self.w2_dram = w1, w2
        self.staged = [ctx.enter_context(nc.semaphore(f"feed_staged{i}")) for i in range(2)]
        self.hi_ready = ctx.enter_context(nc.semaphore("feed_hi_ready"))
        self.lo_ready = ctx.enter_context(nc.semaphore("feed_lo_ready"))

    def words(self, start, count):
        return self.region[:, start:start + count]

    def half(self, m, lo):
        return self.words((2 * (m // 2) + lo) * self.SIZE + (m % 2) * (self.SIZE // 2), self.SIZE // 2)

    def source(self, m):
        n = m // 2
        if n < DC:
            return self.w1_dram[n * P:(n + 1) * P, (m % 2) * FF // 2:(m % 2 + 1) * FF // 2]\
                .rearrange("p (t d) -> p t d", t=2)
        first = (n - DC) * 4 * P + (m % 2) * 2 * P
        return self.w2_dram[first:first + 2 * P, :].rearrange("(f p) d -> p f d", p=P)

    def w1(self, lo, d, f):
        return self.words((2 * d + lo) * self.SIZE + f * P, P)

    def w2(self, lo, f):
        return self.words((2 * (DC + f // 4) + lo) * self.SIZE + (f % 4) * D, D)


def slot_of(att, batch):
    if att == 1 and isinstance(batch, int) and batch == 0:
        return 2
    if att == 2 and isinstance(batch, int) and batch == B - 1:
        return 1
    return att


class Half:

    def __init__(self, att, batch, par, pos, before=None, side=None, ahead=True):
        self.att, self.batch, self.par, self.pos = att, batch, par, pos
        self.before, self.side, self.ahead = before, side, ahead
        self.head0 = pos * H
        self.slot = slot_of(att, batch)
        self.is_first = att == 1 and isinstance(batch, int) and batch == 0
        self.is_second = att == 1 and isinstance(batch, int) and batch == 1
        self.is_last = att == 2 and self.slot == 1
        self.is_before_last = att == 2 and isinstance(batch, int) and batch == B - 2


class Side:

    def __init__(self, att, batch, par):
        self.att, self.batch, self.par = att, batch, par
        self.slot = slot_of(att, batch)
        if att == 1:
            self.first = 0 if isinstance(batch, int) and batch == 0 else 2 * GROUPS * batch - GROUPS
        elif isinstance(batch, int) and batch == B - 1:
            self.first = (2 * B - 1) * GROUPS
        else:
            self.first = 2 * GROUPS * batch + 2 * GROUPS


def first_half(k, par, before=True, side=True, ahead=True):
    return Half(1, k, par, 2 * k - 1,
                before=Half(2, k - 2, par, 2 * k - 2) if before else None,
                side=Side(2, k - 1, 1 - par) if side else None, ahead=ahead)


def second_half(k, par, side=True, ahead=True):
    return Half(2, k, par, 2 * k + 2,
                before=Half(1, k + 1, 1 - par, 2 * k + 1),
                side=Side(1, k + 2, par) if side else None, ahead=ahead)


def at_least(engine, semaphore, value):
    if isinstance(value, int) and value <= 0:
        return
    engine.wait_ge(semaphore, value)


def attention_part(nc, x, adj, adj_t, w, columns, bv1_row, bv2_row, peeled_rows, node_rows, feed):
    with ExitStack() as ctx:
        def sb(name, shape, dt=F32):
            return ctx.enter_context(nc.sbuf_tensor(name, shape, dt))

        def ps(name):
            return ctx.enter_context(nc.psum_tensor(name, [P, 512], F32))

        def sem(name):
            return ctx.enter_context(nc.semaphore(name))

        taken = [0]

        def place(chunks, width):
            start = taken[0]
            taken[0] += chunks * width
            return feed.words(start, chunks * width).rearrange("p (c n) -> p c n", c=chunks)

        w_hi, w_lo = {}, {}
        for n in WEIGHTS:
            w_hi[n], w_lo[n] = place(DC, D), place(DC, D)
        q_hi = {a: sb(f"q{a}_hi", [P, H, N], F32R) for a in (1, 2)}
        q_cross = {a: sb(f"q{a}_cross", [P, H, N], F32R) for a in (1, 2)}
        k_both = {a: sb(f"k{a}_both", [P, H, N], F32R) for a in (1, 2)}
        pe_t_hi, pe_t_lo = [], []
        for i in range(2):
            pe_t_hi.append(place(DC, N))
            pe_t_lo.append(place(DC, N))
        edge_t_hi, edge_t_lo = place(DC, N), place(DC, N)
        v_both = {1: sb("v1", [P, NT, H, P], F32R),
                  2: place(NT, H * P).rearrange("p t (h n) -> p t h n", h=H)}
        pe = [sb(f"pe{i}", [P, NT, D]) for i in range(2)]
        pe_again = sb("pe_again", [P, NT, D])
        adj_raw = sb("adj_raw", [P, NT, N])
        mask = {a: sb(f"mask{a}", [P, NT, N], BF16) for a in (1, 2)}
        probs = sb("probs", [P, NT, N])
        probs_t_hi = sb("probs_t_hi", [P, NT, N], F32R)
        probs_t_lo = sb("probs_t_lo", [P, NT, N], F32R)
        heads_t = sb("heads_t", [P, 2, N])
        rows = {a: sb(f"rows{a}", [P, PAIRS, NT * P]) for a in (1, 2)}
        bv_row = {a: sb(f"bv{a}_row", [P, D]) for a in (1, 2)}
        col = {n: sb(f"{n}_col", [P, DC]) for n in COLUMN_VECTORS}
        ident = sb("ident", [P, P])
        neg_half = sb("neg_half", [P, NT])
        neg_max = sb("neg_max", [P, 2, NT])
        sums = {a: sb(f"sums{a}", [P, NT, H]) for a in (1, 2)}
        inv_sums = sb("inv_sums", [P, NT, H])
        x_stats, row_stats = sb("x_stats", [P, NT, BN_S]), sb("row_stats", [P, NT, BN_S])
        x_mv, row_mv = sb("x_mv", [P, NT, BN_A]), sb("row_mv", [P, NT, BN_A])
        x_var, row_var = sb("x_var", [P, NT]), sb("row_var", [P, NT])
        x_rstd, row_rstd = sb("x_rstd", [P, NT]), sb("row_rstd", [P, NT])
        x_shift = sb("x_shift", [P, NT])
        bias_parts = sb("bias_parts", [P, 2 * DC])

        scores_ps = [ps(f"scores_ps{i}") for i in range(2)]
        probs_t_ps = [ps(f"probs_t_ps{i}") for i in range(2)]
        proj_ps = [ps(f"proj_ps{i}") for i in range(2)]
        heads_ps = ps("heads_ps")
        rows_ps = ps("rows_ps")

        s_columns = sem("columns_loaded")
        s_bv = sem("value_biases_loaded")
        s_stage = [sem(f"weights_staged{i}") for i in range(2)]
        s_w_hi = sem("weights_hi")
        s_w_lo = sem("weights_lo")
        s_w_scaled = sem("weights_scaled")
        s_w_bias = sem("weight_bias_products")
        s_b_bcast = sem("bias_broadcast")
        s_consts = sem("constants_ready")
        s_zeros = sem("zeros_ready")
        s_biases = sem("biases_ready")
        s_x = sem("x_loaded")
        s_x_stats = sem("x_stats_ready")
        s_x_var = sem("x_var_ready")
        s_x_rstd = sem("x_rstd_ready")
        s_x_shift = sem("x_shift_ready")
        s_pe = sem("pe_ready")
        s_pe_stored = sem("pe_stored")
        s_pe_again = sem("pe_again_loaded")
        s_adj = sem("adj_loaded")
        s_mask = sem("mask_ready")
        s_group = sem("proj_group_done")
        s_hi = sem("proj_hi_ready")
        s_lo = sem("proj_lo_ready")
        s_q_crossed = sem("query_hi_crossed")
        s_scores = sem("scores_done")
        s_max = sem("max_ready")
        s_exp = sem("exp_ready")
        s_probs_t = sem("probs_transposed")
        s_pt_hi = sem("probs_t_hi_ready")
        s_pt_lo = sem("probs_t_lo_ready")
        s_pv = sem("values_weighted")
        s_heads_t = sem("heads_t_ready")
        s_rows_ps = sem("rows_transposed")
        s_rows = sem("rows_ready")
        s_inv = sem("inv_sums_ready")
        s_res_step = sem("residual_step")
        s_res = sem("residual_added")
        s_row_stats = sem("row_stats_ready")
        s_row_var = sem("row_var_ready")
        s_row_rstd = sem("row_rstd_ready")
        s_ln = sem("rows_normalised")
        s_node = sem("node_stored")
        s_passed = {e: sem(f"passed_{e}") for e in ("sp", "pool", "dve")}

        HALVES = 2 * len(WEIGHTS)
        CH = DC // 2
        stage = [rows[a][:, :, :].rearrange("p (c a) n -> p c (a n)", c=CH) for a in (1, 2)]

        def mask_number(att, batch):
            if att == 1:
                return 0 if isinstance(batch, int) and batch == 0 else 2 * batch - 1
            if isinstance(batch, int) and batch == B - 1:
                return 2 * B - 1
            return 2 * batch + 2

        def schedule(do_setup, do_project, do_half, do_drain, loop):
            do_setup()
            start = Half(1, 0, 0, 0, side=Side(1, 1, 1), ahead=False)
            do_half(start)
            do_half(Half(1, 1, 1, 1, before=start, ahead=False))
            do_project(Side(2, 0, 0))
            with loop(0, (B - 4) // 2) as i:
                for par in (0, 1):
                    do_half(second_half(2 * i + par, par))
                    do_half(first_half(2 * i + par + 2, par))
            do_half(second_half(B - 4, 0))
            do_half(first_half(B - 2, 0))
            do_half(second_half(B - 3, 1, ahead=False))
            do_half(first_half(B - 1, 1, ahead=False))
            end = second_half(B - 2, 0, side=False, ahead=False)
            do_half(end)
            do_project(Side(2, B - 1, 1))
            last = Half(2, B - 1, 1, 2 * B - 1, before=end, ahead=False)
            do_half(last)
            do_drain(last)

        block = ctx.enter_context(nc.Block())

        @block.sync
        def _(sp):
            def load_x(batch, par):
                hold(sp, s_passed["sp"])
                sp.dma_start(pe[par][:, :, :], x[bass.ds(batch * N, N), :].rearrange(
                    "(t p) d -> p t d", p=P)).then_inc(s_x, 16)

            def load_adj(att, batch):
                src = adj_t if att == 1 else adj
                hold(sp, s_passed["sp"])
                sp.dma_start(adj_raw[:, :, :], src[bass.ds(batch * N, N), :].rearrange(
                    "(t p) n -> p t n", p=P)).then_inc(s_adj, 16)

            def store_pe(batch, par):
                sp.wait_ge(s_pe, batch + 1)
                hold(sp, s_passed["sp"])
                sp.dma_start(peeled_rows[bass.ds(batch * N, N), :].rearrange(
                    "(t p) d -> p t d", p=P), pe[par][:, :, :]).then_inc(s_pe_stored, 16)

            def store_node(half):
                sp.wait_ge(s_ln, half.pos + 1)
                hold(sp, s_passed["sp"])
                for t in range(NT):
                    sp.dma_start(node_rows[bass.ds(half.batch * N + t * P, P), :].rearrange(
                        "p (c n) -> p c n", c=PAIRS), rows[half.slot][:, :, t * P:(t + 1) * P]).then_inc(s_node, 16)
                sp.wait_ge(s_node, (half.batch + 1) * 16 * NT)
                hold(sp, s_passed["sp"])

            def cross_queries(side):
                sp.wait_ge(s_hi, side.first + 5)
                hold(sp, s_passed["sp"])
                for a in range(2):
                    own, other = slice(a * HD, (a + 1) * HD), slice((1 - a) * HD, (2 - a) * HD)
                    sp.dma_start(q_cross[side.slot][other, a::2, :].bitcast(F32),
                                 q_hi[side.slot][own, a::2, :].bitcast(F32)).then_inc(s_q_crossed, 16)

            def load_feed(*halves):
                for m in halves:
                    if m >= 2:
                        sp.wait_ge(feed.hi_ready, m - 1)
                        hold(sp, s_passed["sp"])
                        sp.wait_ge(feed.lo_ready, m - 1)
                        hold(sp, s_passed["sp"])
                    sp.dma_start(pe[m % 2][:, :, :], feed.source(m)).then_inc(feed.staged[m % 2], 16)

            def setup():
                load_x(0, 0)
                for n in COLUMN_VECTORS:
                    sp.dma_start(col[n][:, :], columns[n]).then_inc(s_columns, 16)
                for n in range(HALVES):
                    if n >= 2:
                        sp.wait_ge(s_w_hi, n - 1)
                        hold(sp, s_passed["sp"])
                        sp.wait_ge(s_w_lo, n - 1)
                        hold(sp, s_passed["sp"])
                    src = w[WEIGHTS[n // 2]].rearrange("(c p) o -> p c o", p=P)
                    sp.dma_start(stage[n % 2], src[:, CH * (n % 2):CH * (n % 2) + CH, :]).then_inc(s_stage[n % 2], 16)
                    if n == 5:
                        sp.wait_ge(s_x, 16)
                        load_x(1, 1)
                        load_adj(1, 0)
                        for a, src in ((1, bv1_row), (2, bv2_row)):
                            sp.dma_start(bv_row[a][:, :], src.to_broadcast([P, D])).then_inc(s_bv, 16)
                cross_queries(Side(1, 0, 0))
                sp.wait_ge(s_mask, 1)
                load_adj(1, 1)
                store_pe(0, 0)
                store_pe(1, 1)

            def project(side):
                if side.batch == 0:
                    cross_queries(side)
                    store_pe(2, 0)
                else:
                    load_feed(2, 3)
                    cross_queries(side)
                    load_feed(4, 5)

            def half(h):
                if h.att == 2:
                    if not h.is_last:
                        sp.wait_ge(s_mask, mask_number(2, h.batch + 1))
                        hold(sp, s_passed["sp"])
                        load_adj(2, h.batch + 1)
                    if h.is_last:
                        load_feed(6, 7, 8, 9, 10)
                    sp.wait_ge(s_res, 2 * h.batch + 1)
                    hold(sp, s_passed["sp"])
                    sp.wait_ge(s_pe_stored, (h.batch + 1) * 16)
                    hold(sp, s_passed["sp"])
                    sp.dma_start(pe_again[:, :, :], peeled_rows[bass.ds(h.batch * N, N), :].rearrange(
                        "(t p) d -> p t d", p=P)).then_inc(s_pe_again, 16)
                    if h.ahead:
                        sp.wait_ge(s_res, h.before.pos + 1)
                        hold(sp, s_passed["sp"])
                        sp.wait_ge(s_pe_stored, (h.batch + 2) * 16)
                        hold(sp, s_passed["sp"])
                        sp.wait_ge(s_x, (h.batch + 3) * 16)
                        hold(sp, s_passed["sp"])
                        load_x(h.batch + 3, 1 - h.par)
                    if h.side is not None:
                        cross_queries(h.side)
                    if h.is_before_last:
                        sp.wait_ge(s_res, 2 * B - 2)
                        sp.wait_ge(s_pe_stored, B * 16)
                        load_feed(0, 1)
                    if h.is_last:
                        load_feed(11, 12, 13, 14)
                        store_node(h.before)
                        load_feed(15)
                elif h.is_first:
                    sp.wait_ge(s_mask, 2)
                    hold(sp, s_passed["sp"])
                    load_adj(2, 0)
                    cross_queries(h.side)
                elif h.is_second:
                    sp.wait_ge(s_mask, 3)
                    hold(sp, s_passed["sp"])
                    load_adj(1, 2)
                    sp.wait_ge(s_res, 1)
                    hold(sp, s_passed["sp"])
                    sp.wait_ge(s_pe_stored, 32)
                    hold(sp, s_passed["sp"])
                    load_x(2, 0)
                else:
                    if h.ahead:
                        sp.wait_ge(s_mask, mask_number(1, h.batch + 1))
                        hold(sp, s_passed["sp"])
                        load_adj(1, h.batch + 1)
                    cross_queries(h.side)
                    if h.ahead:
                        store_pe(h.batch + 1, 1 - h.par)
                    store_node(h.before)

            def drain(h):
                store_node(h)

            schedule(setup, project, half, drain, sp.Fori)

        @block.gpsimd
        def _(pool):
            def build_mask(att, batch, head0):
                number = mask_number(att, batch)
                pool.wait_ge(s_adj, (number + 1) * 16)
                at_least(pool, s_max, head0)
                hold(pool, s_passed["pool"])
                pool.tensor_scalar(mask[slot_of(att, batch)][:, :, :], adj_raw[:, :, :], 0.0, MASKED, ALU.is_le, ALU.mult)\
                    .then_inc(s_mask, 1)

            def setup():
                pool.memset(ident[:, :], 0.0).then_inc(s_consts, 1)
                pool.wait_ge(s_consts, 1)
                pool.affine_select(out=ident[:, :], in_=ident[:, :], compare_op=ALU.not_equal, fill=1.0,
                                   base=0, pattern=[[-1, P]], channel_multiplier=1).then_inc(s_consts, 1)
                pool.memset(neg_half[:, :], -0.5).then_inc(s_consts, 1)
                pool.wait_ge(s_consts, 3)
                x_power(0)
                for a in (2, 1):
                    pool.memset(q_hi[a][:, :, :].bitcast(F32), 0.0).then_inc(s_zeros, 1)
                build_mask(1, 0, 0)
                x_power(1)

            def x_power(batch):
                pool.wait_ge(s_x_var, batch + 1)
                pool.tensor_tensor(x_rstd[:, :], x_var[:, :], neg_half[:, :], ALU.pow).then_inc(s_x_rstd, 1)

            def residual(h):
                pool.wait_ge(s_rows, (h.pos + 1) * PAIRS)
                pool.wait_ge(s_inv, h.pos + 1)
                if h.att == 2:
                    pool.wait_ge(s_pe_again, (h.batch + 1) * 16)
                src = pe_again if h.att == 2 else pe[h.par]
                for t in range(NT):
                    r = rows[h.slot][:, :, t * P:(t + 1) * P]
                    heads = r.rearrange("p c (a d) -> p c a d", a=2)
                    inv = inv_sums[:, t, :].rearrange("p (c a) -> p c a", a=2).unsqueeze(3)\
                        .to_broadcast([P, PAIRS, 2, HD])
                    pool.tensor_tensor(heads, heads, inv, ALU.mult).then_inc(s_res_step, 1)
                for t in range(NT):
                    r = rows[h.slot][:, :, t * P:(t + 1) * P]
                    add = src[:, t, :].rearrange("p (c n) -> p c n", c=PAIRS)
                    pool.wait_ge(s_res_step, 4 * h.pos + t + 1)
                    pool.tensor_tensor(r, r, add, ALU.add).then_inc(s_res_step, 1)
                for t in range(NT):
                    r = rows[h.slot][:, :, t * P:(t + 1) * P]
                    bias = bv_row[h.att][:, :].rearrange("p (c n) -> p c n", c=PAIRS)
                    pool.wait_ge(s_res_step, 4 * h.pos + NT + t + 1)
                    add = pool.tensor_tensor(r, r, bias, ALU.add)
                add.then_inc(s_res, 1)

            def row_power(h):
                pool.wait_ge(s_row_var, h.pos + 1)
                pool.tensor_tensor(row_rstd[:, :], row_var[:, :], neg_half[:, :], ALU.pow).then_inc(s_row_rstd, 1)

            def project(side):
                if side.batch == 0:
                    x_power(2)
                else:
                    build_mask(2, B - 1, H * (2 * B - 2))

            def half(h):
                if h.is_first:
                    build_mask(1, 1, 0)
                elif h.is_second:
                    build_mask(2, 0, h.head0)
                elif h.side is not None:
                    if h.att == 2:
                        build_mask(1, h.batch + 2, h.head0)
                    else:
                        build_mask(2, h.batch - 1, h.head0)
                if h.att == 1 and h.ahead:
                    x_power(h.batch + 1)
                if h.before is not None:
                    residual(h.before)
                if h.before is not None:
                    row_power(h.before)

            def drain(h):
                residual(h)
                row_power(h)

            schedule(setup, project, half, drain, pool.Fori)

        @block.tensor
        def _(pe_eng):
            mm, tr = pe_eng.matmul, pe_eng.transpose

            def three(out, stat_hi, stat_lo, mov_hi, mov_lo, first, last):
                mm(out, stat_hi, mov_hi, start=first, stop=False)
                mm(out, stat_hi, mov_lo, start=False, stop=False)
                return mm(out, stat_lo, mov_hi, start=False, stop=last)

            def group_ready(side, j, m):
                at_least(pe_eng, s_hi, m - 1)
                at_least(pe_eng, s_lo, m - 1)
                if j == 0:
                    if side.att == 1:
                        pe_eng.wait_ge(s_pe, side.batch + 1)
                    elif isinstance(side.batch, int) and side.batch == 0:
                        pe_eng.wait_ge(s_ln, 1)
                    else:
                        pe_eng.wait_ge(s_ln, 2 * side.batch)

            def side_piece(side, j, c):
                m, bank = side.first + j, proj_ps[j % 2]
                if c == 0:
                    group_ready(side, j, m)
                last = None
                if j < 2:
                    chunk = 2 * j + c
                    for t in range(NT):
                        src = pe[side.par][:, t, chunk * P:(chunk + 1) * P] if side.att == 1 else \
                            rows[slot_of(1, side.batch)][:, chunk, t * P:(t + 1) * P]
                        last = tr(bank[:, c * N + t * P:c * N + (t + 1) * P], src, ident[:, :])
                elif j < 6:
                    names = ("n2e_q_w", "n2e_k_w") if side.att == 1 else ("e2n_q_w", "e2n_k_w")
                    name = names[j % 2]
                    edge = side.att == 2 and j % 2 == 1
                    hi, lo = (edge_t_hi, edge_t_lo) if edge else (pe_t_hi[side.par], pe_t_lo[side.par])
                    o = (2 * ((j - 2) // 2) + c) * P
                    for d in range(DC):
                        if (j, c, d) == (2, 0, 2):
                            pe_eng.wait_ge(s_hi, side.first + 2)
                            pe_eng.wait_ge(s_lo, side.first + 2)
                        last = three(bank[:, c * N:(c + 1) * N], w_hi[name][:, d, o:o + P], w_lo[name][:, d, o:o + P],
                                     hi[:, d, :], lo[:, d, :], d == 0, d == DC - 1)
                else:
                    name = "n2e_v_w" if side.att == 1 else "e2n_v_w"
                    hi, lo = (edge_t_hi, edge_t_lo) if side.att == 2 else (pe_t_hi[side.par], pe_t_lo[side.par])
                    t = j - 6
                    for d in range(2 * c, 2 * c + 2):
                        last = three(bank[:, :], hi[:, d, t * P:(t + 1) * P], lo[:, d, t * P:(t + 1) * P],
                                     w_hi[name][:, d, :], w_lo[name][:, d, :], d == 0, d == DC - 1)
                if c == 1:
                    last.then_inc(s_group, 1)

            def scores(h, u):
                g = h.head0 + u
                if u == 0:
                    first = Side(h.att, h.batch, h.par).first
                    pe_eng.wait_ge(s_hi, first + 6)
                    pe_eng.wait_ge(s_lo, first + 6)
                    pe_eng.wait_ge(s_q_crossed, 32 * (h.pos + 1))
                at_least(pe_eng, s_exp, g - 1)
                for t in range(NT):
                    out, q = scores_ps[u % 2][:, t * N:(t + 1) * N], (slice(None), u, slice(t * P, (t + 1) * P))
                    mm(out, q_cross[h.slot][q], k_both[h.slot][:, u, :], start=True, stop=False)
                    last = mm(out, q_hi[h.slot][q], k_both[h.slot][:, u, :], start=False, stop=True)
                last.then_inc(s_scores, 1)

            def transpose_probs(h, u):
                g = h.head0 + u
                pe_eng.wait_ge(s_exp, g + 1)
                for j in range(NT):
                    for t in range(NT):
                        last = tr(probs_t_ps[u % 2][:, j * N + t * P:j * N + (t + 1) * P],
                                  probs[:, t, j * P:(j + 1) * P], ident[:, :])
                last.then_inc(s_probs_t, 1)

            def weigh_values(h, u):
                g = h.head0 + u
                if u == 0:
                    first = Side(h.att, h.batch, h.par).first
                    pe_eng.wait_ge(s_hi, first + GROUPS)
                    pe_eng.wait_ge(s_lo, first + GROUPS)
                if u % 2 == 0:
                    at_least(pe_eng, s_heads_t, h.pos * PAIRS + u // 2)
                pe_eng.wait_ge(s_pt_hi, g + 1)
                pe_eng.wait_ge(s_pt_lo, g + 1)
                out = heads_ps[:, (u % 2) * N:(u % 2 + 1) * N]
                for j in range(NT):
                    mm(out, v_both[h.slot][:, j, u, :], probs_t_hi[:, j, :], start=j == 0, stop=False)
                    last = mm(out, v_both[h.slot][:, j, u, :], probs_t_lo[:, j, :], start=False, stop=j == NT - 1)
                last.then_inc(s_pv, 1)

            def transpose_heads(h, p):
                pair = h.pos * PAIRS + p
                pe_eng.wait_ge(s_heads_t, pair + 1)
                at_least(pe_eng, s_rows, pair)
                for t in range(NT):
                    for a in range(2):
                        o = (t * 2 + a) * P
                        last = tr(rows_ps[:, o:o + P], heads_t[:, a, t * P:(t + 1) * P], ident[:, :])
                last.then_inc(s_rows_ps, 1)

            def bias_product(n):
                pe_eng.wait_ge(s_stage[n % 2], 16 * (n // 2 + 1))
                raw = stage[n % 2]
                if n < HALVES - 2:
                    pe_eng.wait_ge(s_columns, 16 * len(COLUMN_VECTORS))
                    for o in range(DC):
                        for c in range(CH):
                            d = CH * (n % 2) + c
                            last = mm(scores_ps[n % 2][:, o:o + 1], raw[:, c, o * P:(o + 1) * P],
                                      col["norm1_b"][:, d:d + 1], start=c == 0, stop=c == CH - 1)
                else:
                    pe_eng.wait_ge(s_b_bcast, 1)
                    for c in range(CH):
                        d = CH * (n % 2) + c
                        last = mm(heads_ps[:, :], probs[:, :, :].rearrange("p t n -> p (t n)")[:, d * P:(d + 1) * P],
                                  raw[:, c, :], start=d == 0, stop=d == DC - 1)
                last.then_inc(s_w_bias, 1)

            def setup():
                pe_eng.wait_ge(s_consts, 2)
                side = Side(1, 0, 0)
                for what, n in SETUP_ORDER:
                    if what == "g":
                        if n in (2, 3, 6):
                            pe_eng.wait_ge(s_w_hi, {2: 2, 3: 4, 6: 6}[n])
                            pe_eng.wait_ge(s_w_lo, {2: 2, 3: 4, 6: 6}[n])
                        side_piece(side, n, 0)
                        side_piece(side, n, 1)
                    elif n >= HALVES - 4:
                        bias_product(n)
                pe_eng.wait_ge(s_w_hi, HALVES)
                pe_eng.wait_ge(s_w_lo, HALVES)
                pe_eng.wait_ge(s_biases, 2)

            def project(side):
                for j in range(GROUPS):
                    side_piece(side, j, 0)
                    side_piece(side, j, 1)

            def half(h):
                for u in range(H):
                    scores(h, u)
                    if u == 0 and h.side is not None:
                        for j, c in SIDE_PIECES[u][0]:
                            side_piece(h.side, j, c)
                    if u % 2 == 0 and u >= 4:
                        transpose_heads(h, u // 2 - 2)
                    elif u % 2 == 0 and h.before is not None:
                        transpose_heads(h.before, PAIRS - 2 + u // 2)
                    if u and h.side is not None:
                        for j, c in SIDE_PIECES[u][0]:
                            side_piece(h.side, j, c)
                    if u >= 2:
                        weigh_values(h, u - 2)
                    elif h.before is not None:
                        weigh_values(h.before, H - 2 + u)
                    if u:
                        transpose_probs(h, u - 1)
                    elif h.before is not None:
                        transpose_probs(h.before, H - 1)
                    if h.side is not None:
                        for j, c in SIDE_PIECES[u][1]:
                            side_piece(h.side, j, c)

            def drain(h):
                transpose_heads(h, PAIRS - 2)
                weigh_values(h, H - 2)
                transpose_probs(h, H - 1)
                weigh_values(h, H - 1)
                transpose_heads(h, PAIRS - 1)

            schedule(setup, project, half, drain, pe_eng.Fori)

        @block.scalar
        def _(act):
            def project_hi(side, j):
                m, bank = side.first + j, proj_ps[j % 2]
                act.wait_ge(s_group, m + 1)
                if j < 2:
                    dst = pe_t_hi[side.par] if side.att == 1 else edge_t_hi
                    act.activation(dst[:, 2 * j:2 * j + 2, :].rearrange("p c n -> p (c n)"), bank[:, :], ACT.Copy)\
                        .then_inc(s_hi, 1)
                elif j < 6:
                    pair0 = 2 * ((j - 2) // 2)
                    for c in range(2):
                        src, ch = bank[:, c * N:(c + 1) * N], pair0 + c
                        dst = k_both if j % 2 else q_hi
                        name = ("n2e" if side.att == 1 else "e2n") + ("_k_b" if j % 2 else "_q_b")
                        for a in range(2):
                            s = slice(a * HD, (a + 1) * HD)
                            last = act.activation(dst[side.slot][s, 2 * ch + a, :], src[s, :], ACT.Identity,
                                                  bias=col[name][s, ch:ch + 1])
                    last.then_inc(s_hi, 1)
                else:
                    t = j - 6
                    act.activation(v_both[side.slot][:, t, :, 0:HD], bank[:, :].rearrange("p (h d) -> p h d", h=H),
                                   ACT.Copy).then_inc(s_hi, 1)

            def exps(h, u):
                g = h.head0 + u
                act.wait_ge(s_max, g + 1)
                at_least(act, s_probs_t, g)
                for t in range(NT):
                    last = act.activation(probs[:, t, :], scores_ps[u % 2][:, t * N:(t + 1) * N], ACT.Exp,
                                          bias=neg_max[:, u % 2, t:t + 1], scale=-1.0,
                                          accum_out=sums[h.slot][:, t, u:u + 1])
                last.then_inc(s_exp, 1)

            def probs_hi(h, u):
                g = h.head0 + u
                act.wait_ge(s_probs_t, g + 1)
                at_least(act, s_pv, g)
                act.activation(probs_t_hi[:, :, :].rearrange("p t n -> p (t n)"), probs_t_ps[u % 2][:, :], ACT.Copy)\
                    .then_inc(s_pt_hi, 1)

            def heads_out(h, p):
                pair = h.pos * PAIRS + p
                act.wait_ge(s_pv, h.head0 + 2 * p + 2)
                at_least(act, s_rows_ps, pair)
                act.activation(heads_t[:, :, :].rearrange("p a n -> p (a n)"), heads_ps[:, :], ACT.Copy)\
                    .then_inc(s_heads_t, 1)

            def x_relu(batch, par):
                act.wait_ge(s_x_shift, batch + 1)
                for t in range(NT):
                    last = act.activation(pe[par][:, t, :], pe[par][:, t, :], ACT.Relu,
                                          bias=x_shift[:, t:t + 1], scale=x_rstd[:, t:t + 1])
                last.then_inc(s_pe, 1)

            def weight_hi(n):
                name = WEIGHTS[n // 2]
                if n < HALVES - 4:
                    act.wait_ge(s_stage[n % 2], 16 * (n // 2 + 1))
                else:
                    act.wait_ge(s_w_scaled, n - (HALVES - 4) + 1)
                act.activation(w_hi[name][:, CH * (n % 2):CH * (n % 2) + CH, :], stage[n % 2], ACT.Copy)\
                    .then_inc(s_w_hi, 1)

            def setup():
                act.wait_ge(s_columns, 16 * len(COLUMN_VECTORS))
                for what, n in SETUP_ORDER:
                    if what == "w":
                        weight_hi(n)
                        if n == 0:
                            x_relu(0, 0)
                        elif n == 7:
                            x_relu(1, 1)
                    else:
                        if n == 2:
                            act.wait_ge(s_zeros, 2)
                        project_hi(Side(1, 0, 0), n)
                act.wait_ge(s_biases, 2)

            def feed_hi(m):
                act.wait_ge(feed.staged[m % 2], 16 * (m // 2 + 1))
                act.activation(feed.half(m, 0), pe[m % 2][:, :, :].rearrange("p t d -> p (t d)"), ACT.Copy)\
                    .then_inc(feed.hi_ready, 1)

            def project(side):
                for j in range(GROUPS):
                    project_hi(side, j)
                    if side.batch == 0 and j == 3:
                        x_relu(2, 0)
                    if side.batch == B - 1 and j in feed.AT_GROUPS:
                        feed_hi(feed.AT_GROUPS[j])

            def half(h):
                for u in range(H):
                    if h.side is not None:
                        for j in SIDE_SPLITS[u]:
                            project_hi(h.side, j)
                    if u >= 3 and u % 2:
                        heads_out(h, (u - 3) // 2)
                    elif u == 1 and h.before is not None:
                        heads_out(h.before, PAIRS - 1)
                    if u:
                        probs_hi(h, u - 1)
                    elif h.before is not None:
                        probs_hi(h.before, H - 1)
                    exps(h, u)
                    if u == 5 and h.att == 1 and h.ahead:
                        x_relu(h.batch + 1, 1 - h.par)
                    if h.is_before_last and u in feed.AT_HEADS_BEFORE:
                        feed_hi(feed.AT_HEADS_BEFORE[u])
                    if h.is_last:
                        feed_hi(feed.AT_HEADS_LAST[u])

            def drain(h):
                probs_hi(h, H - 1)
                heads_out(h, PAIRS - 1)
                for m in feed.AT_END:
                    feed_hi(m)

            schedule(setup, project, half, drain, act.Fori)

        @block.vector
        def _(dve):
            def project_lo(side, j):
                m, bank = side.first + j, proj_ps[j % 2]
                dve.wait_ge(s_hi, m + 1)
                if j < 2:
                    hi, lo = (pe_t_hi[side.par], pe_t_lo[side.par]) if side.att == 1 else (edge_t_hi, edge_t_lo)
                    s = (slice(None), slice(2 * j, 2 * j + 2), slice(None))
                    dve.tensor_tensor(lo[s].rearrange("p c n -> p (c n)"), bank[:, :],
                                      hi[s].rearrange("p c n -> p (c n)").bitcast(F32), ALU.subtract).then_inc(s_lo, 1)
                elif j < 6:
                    pair0 = 2 * ((j - 2) // 2)
                    for c in range(2):
                        src, ch = bank[:, c * N:(c + 1) * N], pair0 + c
                        hi = k_both if j % 2 else q_hi
                        name = ("n2e" if side.att == 1 else "e2n") + ("_k_b" if j % 2 else "_q_b")
                        for a in range(2):
                            s, head = slice(a * HD, (a + 1) * HD), 2 * ch + a
                            other = slice((1 - a) * HD, (2 - a) * HD)
                            lo = k_both[side.slot][other, head, :] if j % 2 else q_cross[side.slot][s, head, :]
                            last = dve.scalar_tensor_tensor(lo, src[s, :], col[name][s, ch:ch + 1],
                                                            hi[side.slot][s, head, :].bitcast(F32),
                                                            ALU.add, ALU.subtract)
                    last.then_inc(s_lo, 1)
                else:
                    t = j - 6
                    v = v_both[side.slot]
                    dve.tensor_tensor(v[:, t, :, HD:P], bank[:, :].rearrange("p (h d) -> p h d", h=H),
                                      v[:, t, :, 0:HD].bitcast(F32), ALU.subtract).then_inc(s_lo, 1)

            def maxima(h, u):
                g = h.head0 + u
                if u == 0:
                    dve.wait_ge(s_mask, mask_number(h.att, h.batch) + 1)
                dve.wait_ge(s_scores, g + 1)
                hold(dve, s_passed["dve"])
                for t in range(NT):
                    s = scores_ps[u % 2][:, t * N:(t + 1) * N]
                    last = dve.tensor_tensor_reduce(s, s, mask[h.slot][:, t, :], -SCALE, 3e38, ALU.add, ALU.min,
                                                    neg_max[:, u % 2, t:t + 1])
                last.then_inc(s_max, 1)

            def probs_lo(h, u):
                g = h.head0 + u
                dve.wait_ge(s_pt_hi, g + 1)
                dve.tensor_tensor(probs_t_lo[:, :, :].rearrange("p t n -> p (t n)"), probs_t_ps[u % 2][:, :],
                                  probs_t_hi[:, :, :].rearrange("p t n -> p (t n)").bitcast(F32), ALU.subtract)\
                    .then_inc(s_pt_lo, 1)

            def head_rows(h, p):
                pair = h.pos * PAIRS + p
                if p == 0 and h.att == 2 and not h.is_last:
                    dve.wait_ge(s_pe_again, (h.batch + 1) * 16)
                dve.wait_ge(s_rows_ps, pair + 1)
                dve.tensor_reduce(rows[h.slot][:, p, :].rearrange("p (a d) -> p a d", a=4),
                                  rows_ps[:, :].rearrange("p (a x d) -> p a d x", a=4, x=2), AX_X, ALU.add)\
                    .then_inc(s_rows, 1)

            def inverse_sums(h):
                dve.wait_ge(s_exp, h.head0 + H)
                dve.reciprocal(inv_sums[:, :, :].rearrange("p t h -> p (t h)"),
                               sums[h.slot][:, :, :].rearrange("p t h -> p (t h)")).then_inc(s_inv, 1)

            def moments(src, stats, mv, var, s_stats, s_var, count):
                for t in range(NT):
                    dve.bn_stats(stats[:, t, :], src(t)).then_inc(s_stats, 1)
                for t in range(NT):
                    dve.wait_ge(s_stats, count * 2 * NT + t + 1)
                    hold(dve, s_passed["dve"])
                    dve.bn_aggr(mv[:, t, :], stats[:, t, :]).then_inc(s_stats, 1)
                dve.wait_ge(s_stats, count * 2 * NT + 2 * NT)
                dve.tensor_scalar(var[:, :], mv[:, :, 1], LN_EPS, None, ALU.add).then_inc(s_var, 1)

            def x_moments(batch, par):
                dve.wait_ge(s_x, (batch + 1) * 16)
                moments(lambda t: pe[par][:, t, :], x_stats, x_mv, x_var, s_x_stats, s_x_var, batch)

            def x_shifts(batch):
                dve.wait_ge(s_x_rstd, batch + 1)
                dve.scalar_tensor_tensor(x_shift[:, :], x_mv[:, :, 0], -1.0, x_rstd[:, :], ALU.mult, ALU.mult)\
                    .then_inc(s_x_shift, 1)

            def row_moments(h):
                dve.wait_ge(s_res, h.pos + 1)
                moments(lambda t: rows[h.slot][:, :, t * P:(t + 1) * P], row_stats, row_mv, row_var,
                        s_row_stats, s_row_var, h.pos)

            def normalise(h):
                dve.wait_ge(s_row_rstd, h.pos + 1)
                for t in range(NT):
                    r = rows[h.slot][:, :, t * P:(t + 1) * P]
                    last = dve.tensor_scalar(r, r, row_mv[:, t, 0:1], row_rstd[:, t:t + 1], ALU.subtract, ALU.mult)
                last.then_inc(s_ln, 1)

            def weight_lo(n):
                name = WEIGHTS[n // 2]
                if n >= HALVES - 4:
                    k = n - (HALVES - 4)
                    dve.wait_ge(s_stage[n % 2], 16 * (n // 2 + 1))
                    dve.wait_ge(s_w_bias, k + 1)
                    for c in range(CH):
                        d = CH * (n % 2) + c
                        last = dve.tensor_scalar(stage[n % 2][:, c, :], stage[n % 2][:, c, :],
                                                 col["norm1_g"][:, d:d + 1], None, ALU.mult)
                    last.then_inc(s_w_scaled, 1)
                dve.wait_ge(s_w_hi, n + 1)
                s = (slice(None), slice(CH * (n % 2), CH * (n % 2) + CH), slice(None))
                dve.tensor_tensor(w_lo[name][s], stage[n % 2], w_hi[name][s].bitcast(F32), ALU.subtract)\
                    .then_inc(s_w_lo, 1)

            def setup():
                dve.wait_ge(s_columns, 16 * len(COLUMN_VECTORS))
                x_moments(0, 0)
                x_shifts(0)
                for c in range(DC):
                    last = dve.tensor_copy(probs[:, :, :].rearrange("p t n -> p (t n)")[:, c * P:(c + 1) * P],
                                           col["norm1_b"][:, c:c + 1].to_broadcast([P, P]))
                last.then_inc(s_b_bcast, 1)
                for what, n in SETUP_ORDER:
                    if what == "w":
                        weight_lo(n)
                        if n == 6:
                            dve.wait_ge(s_pe, 1)
                            x_moments(1, 1)
                            x_shifts(1)
                    else:
                        project_lo(Side(1, 0, 0), n)
                dve.tensor_copy(bias_parts[:, 0:DC], scores_ps[0][:, 0:DC]).then_inc(s_biases, 1)
                dve.wait_ge(s_biases, 1)
                dve.tensor_tensor(bias_parts[:, DC:2 * DC], scores_ps[1][:, 0:DC], bias_parts[:, 0:DC], ALU.add)\
                    .then_inc(s_b_bcast, 1)
                dve.wait_ge(s_b_bcast, 2)
                dve.tensor_tensor(col["e2n_k_b"][:, :], col["e2n_k_b"][:, :], bias_parts[:, DC:2 * DC], ALU.add)\
                    .then_inc(s_b_bcast, 1)
                dve.wait_ge(s_bv, 32)
                dve.tensor_tensor(bv_row[2][:, :], heads_ps[:, :], bv_row[2][:, :], ALU.add).then_inc(s_b_bcast, 1)
                dve.wait_ge(s_b_bcast, 4)
                dve.tensor_copy(bias_parts[:, 0:1], neg_half[:, 0:1]).then_inc(s_biases, 1)

            def feed_lo(m):
                dve.wait_ge(feed.hi_ready, m + 1)
                dve.tensor_tensor(feed.half(m, 1), pe[m % 2][:, :, :].rearrange("p t d -> p (t d)"),
                                  feed.half(m, 0).bitcast(F32), ALU.subtract).then_inc(feed.lo_ready, 1)

            def project(side):
                for j in range(GROUPS):
                    project_lo(side, j)
                    if side.batch == B - 1 and j in feed.AT_GROUPS:
                        feed_lo(feed.AT_GROUPS[j])
                    if side.batch == 0 and j == 1:
                        x_moments(2, 0)
                    if side.batch == 0 and j == 2:
                        x_shifts(2)

            def half(h):
                for u in range(H):
                    maxima(h, u)
                    if h.side is not None:
                        for j in SIDE_SPLITS[u]:
                            project_lo(h.side, j)
                    if u % 2 == 0 and u >= 4:
                        head_rows(h, u // 2 - 2)
                    elif u == 2 and h.before is not None:
                        head_rows(h.before, PAIRS - 1)
                    if u:
                        probs_lo(h, u - 1)
                    elif h.before is not None:
                        probs_lo(h.before, H - 1)
                        head_rows(h.before, PAIRS - 2)
                    if h.att == 1 and h.ahead:
                        if u == 1:
                            x_moments(h.batch + 1, 1 - h.par)
                        if u == 2:
                            x_shifts(h.batch + 1)
                    if h.before is not None:
                        if u == 1:
                            inverse_sums(h.before)
                        if u == 4:
                            row_moments(h.before)
                        if u == 6:
                            normalise(h.before)
                    if h.is_before_last and u in feed.AT_HEADS_BEFORE:
                        feed_lo(feed.AT_HEADS_BEFORE[u])
                    if h.is_last:
                        feed_lo(feed.AT_HEADS_LAST[u])

            def drain(h):
                head_rows(h, PAIRS - 2)
                probs_lo(h, H - 1)
                inverse_sums(h)
                head_rows(h, PAIRS - 1)
                for m in feed.AT_END:
                    feed_lo(m)
                row_moments(h)
                normalise(h)

            schedule(setup, project, half, drain, dve.Fori)


def feed_forward_part(nc, x, node_rows, feed, gain2_col, bias2_col, b1_col, row_vectors, out):
    with ExitStack() as ctx:
        def sb(name, shape, dt=F32):
            return ctx.enter_context(nc.sbuf_tensor(name, shape, dt))

        def ps(name):
            return ctx.enter_context(nc.psum_tensor(name, [P, 512], F32))

        def sem(name):
            return ctx.enter_context(nc.semaphore(name))

        z = [sb(f"z{i}", [P, RT, D]) for i in range(2)]
        xr = [sb(f"xr{i}", [P, RT, D]) for i in range(2)]
        z_t = [sb(f"z_t{i}", [P, ROWS]) for i in range(2)]
        z_t_hi, z_t_lo = sb("z_t_hi", [P, DC, ROWS], F32R), sb("z_t_lo", [P, DC, ROWS], F32R)
        hid = [sb(f"hid{i}", [P, ROWS]) for i in range(2)]
        hid_hi = [sb(f"hid_hi{i}", [P, ROWS], F32R) for i in range(2)]
        hid_lo = [sb(f"hid_lo{i}", [P, ROWS], F32R) for i in range(2)]
        gain2, bias2, gain3, bias3, b2_row = (sb(n, [P, D]) for n in ("gain2", "bias2", "gain3", "bias3", "b2_row"))
        gain2_c, bias2_c, b1_c = sb("gain2_c", [P, DC]), sb("bias2_c", [P, DC]), sb("b1_c", [P, FT])
        ident2 = sb("ident2", [P, P])
        neg_half2 = sb("neg_half2", [P, RT])
        stats, mv = sb("stats", [P, RT, BN_S]), sb("mv", [P, RT, BN_A])
        var, rstd = sb("var", [P, RT]), sb("rstd", [P, RT])

        hid_ps = [ps(f"hid_ps{i}") for i in range(2)]
        t_ps = [ps(f"t_ps{i}") for i in range(2)]
        out_ps = [ps(f"out_ps{i}") for i in range(RT)]

        f_passed = {e: sem(f"ff_passed_{e}") for e in ("sp", "dve")}
        f_columns = sem("ff_columns_loaded")
        f_vec = sem("ff_rows_loaded")
        f_const = sem("ff_constants")
        f_b2 = sem("ff_b2_ready")
        f_z = [sem(f"z_loaded{i}") for i in range(2)]
        f_x = [sem(f"x_again_loaded{i}") for i in range(2)]
        f_t = sem("z_transposed")
        f_t_raw = sem("z_t_ready")
        f_t_hi = sem("z_t_hi_ready")
        f_t_lo = sem("z_t_lo_ready")
        f_hid_ps = sem("hid_done")
        f_hid = sem("gelu_ready")
        f_hid_hi = sem("hid_hi_ready")
        f_hid_lo = sem("hid_lo_ready")
        f_hid_used = sem("hid_used")
        f_node_step = sem("node_step")
        f_node = sem("node_features_ready")
        f_x_bias = sem("x_biased")
        f_out_ps = sem("out_done")
        f_sum = sem("sum_ready")
        f_stats = sem("ff_stats")
        f_var = sem("ff_var")
        f_rstd = sem("ff_rstd")
        f_norm = sem("ff_normalised")
        f_gain = sem("ff_gain")
        f_final = sem("ff_final")
        f_stored = [sem(f"out_stored{i}") for i in range(2)]

        def schedule(do_setup, do_pass, loop):
            do_setup()
            do_pass(0, 0, 0)
            do_pass(1, 1, 0)
            with loop(1, PASSES // 2 - 1) as i:
                do_pass(2 * i, 0, i)
                do_pass(2 * i + 1, 1, i)
            do_pass(PASSES - 2, 0, PASSES // 2 - 1)
            do_pass(PASSES - 1, 1, PASSES // 2 - 1, last=True)

        block = ctx.enter_context(nc.Block())

        @block.sync
        def _(sp):
            def load(dst, src, r, s):
                hold(sp, f_passed["sp"])
                sp.dma_start(dst[:, :, :], src[bass.ds(r * ROWS, ROWS), :].rearrange(
                    "(t p) d -> p t d", p=P)).then_inc(s, 16)

            def setup():
                load(z[0], node_rows, 0, f_z[0])
                for dst, src in ((gain2_c, gain2_col), (bias2_c, bias2_col), (b1_c, b1_col)):
                    sp.dma_start(dst[:, :], src).then_inc(f_columns, 16)
                load(xr[0], x, 0, f_x[0])
                for dst, src in zip((gain2, bias2, gain3, bias3, b2_row), row_vectors):
                    sp.dma_start(dst[:, :], src.to_broadcast([P, D])).then_inc(f_vec, 16)

            def do_pass(r, par, i, last=False):
                if not last:
                    nxt = 1 - par
                    if not (isinstance(r, int) and r == 0):
                        sp.wait_ge(f_final, r * RT)
                        hold(sp, f_passed["sp"])
                        sp.wait_ge(f_stored[nxt], (i + par) * RT * 16)
                        hold(sp, f_passed["sp"])
                    load(z[nxt], node_rows, r + 1, f_z[nxt])
                    load(xr[nxt], x, r + 1, f_x[nxt])
                for t in range(RT):
                    sp.wait_ge(f_final, r * RT + t + 1)
                    hold(sp, f_passed["sp"])
                    sp.dma_start(out[bass.ds(r * ROWS + t * P, P), :], xr[par][:, t, :]).then_inc(f_stored[par], 16)
                if isinstance(r, int) and r >= PASSES - 2:
                    sp.wait_ge(f_stored[par], (i + 1) * RT * 16)
                    hold(sp, f_passed["sp"])

            schedule(setup, do_pass, sp.Fori)

        @block.gpsimd
        def _(pool):
            def setup():
                pool.memset(ident2[:, :], 0.0).then_inc(f_const, 1)
                pool.wait_ge(f_const, 1)
                pool.affine_select(out=ident2[:, :], in_=ident2[:, :], compare_op=ALU.not_equal, fill=1.0,
                                   base=0, pattern=[[-1, P]], channel_multiplier=1).then_inc(f_const, 1)
                pool.memset(neg_half2[:, :], -0.5).then_inc(f_const, 1)
                pool.wait_ge(f_vec, 16 * 5)
                pool.tensor_tensor(bias2[:, :], bias2[:, :], b2_row[:, :], ALU.add).then_inc(f_b2, 1)
                pool.wait_ge(f_b2, 1)
                pool.wait_ge(f_const, 3)

            def finish(r, par):
                for t in range(RT):
                    pool.wait_ge(f_norm, r * RT + t + 1)
                    pool.tensor_tensor(z[par][:, t, :], z[par][:, t, :], gain3[:, :], ALU.mult).then_inc(f_gain, 1)
                for t in range(RT):
                    pool.wait_ge(f_gain, r * RT + t + 1)
                    pool.tensor_tensor(xr[par][:, t, :], xr[par][:, t, :], z[par][:, t, :], ALU.add)\
                        .then_inc(f_final, 1)

            def power(r):
                pool.wait_ge(f_var, r + 1)
                pool.tensor_tensor(rstd[:, :], var[:, :], neg_half2[:, :], ALU.pow).then_inc(f_rstd, 1)

            def do_pass(r, par, i, last=False):
                if not (isinstance(r, int) and r == 0):
                    power(r - 1)
                    finish(r - 1, 1 - par)
                pool.wait_ge(f_x[par], (i + 1) * 16)
                for t in range(RT):
                    pool.tensor_tensor(xr[par][:, t, :], xr[par][:, t, :], bias3[:, :], ALU.add).then_inc(f_x_bias, 1)
                pool.wait_ge(f_z[par], (i + 1) * 16)
                pool.wait_ge(f_t, r * DC + DC)
                for t in range(RT):
                    pool.tensor_tensor(z[par][:, t, :], z[par][:, t, :], gain2[:, :], ALU.mult).then_inc(f_node_step, 1)
                for t in range(RT):
                    pool.wait_ge(f_node_step, r * RT + t + 1)
                    pool.tensor_tensor(z[par][:, t, :], z[par][:, t, :], bias2[:, :], ALU.add).then_inc(f_node, 1)
                pool.wait_ge(f_x_bias, (r + 1) * RT)
                if last:
                    power(r)
                    finish(r, par)

            schedule(setup, do_pass, pool.Fori)

        @block.tensor
        def _(pe_eng):
            mm, tr = pe_eng.matmul, pe_eng.transpose

            def transpose_rows(r, par, i, c):
                if c == 0:
                    pe_eng.wait_ge(f_z[par], (i + 1) * 16)
                if not (isinstance(r, int) and r == 0 and c < 2):
                    pe_eng.wait_ge(f_t_raw, r * DC + c - 1)
                for t in range(RT):
                    last = tr(t_ps[c % 2][:, t * P:(t + 1) * P], z[par][:, t, c * P:(c + 1) * P], ident2[:, :])
                last.then_inc(f_t, 1)

            def hidden(r, f):
                n = r * FT + f
                if f == 0:
                    pe_eng.wait_ge(f_t_hi, (r + 1) * DC)
                    pe_eng.wait_ge(f_t_lo, (r + 1) * DC)
                if not (isinstance(r, int) and r == 0 and f < 2):
                    pe_eng.wait_ge(f_hid, n - 1)
                o = hid_ps[f % 2][:, :]
                for d in range(DC):
                    mm(o, feed.w1(0, d, f), z_t_hi[:, d, :], start=d == 0, stop=False)
                    mm(o, feed.w1(0, d, f), z_t_lo[:, d, :], start=False, stop=False)
                    last = mm(o, feed.w1(1, d, f), z_t_hi[:, d, :], start=False, stop=d == DC - 1)
                last.then_inc(f_hid_ps, 1)

            def outcome(r, f):
                n = r * FT + f
                pe_eng.wait_ge(f_hid_hi, n + 1)
                pe_eng.wait_ge(f_hid_lo, n + 1)
                for t in range(RT):
                    if f == 0 and not (isinstance(r, int) and r == 0):
                        pe_eng.wait_ge(f_sum, (r - 1) * RT + t + 1)
                    s = slice(t * P, (t + 1) * P)
                    o = out_ps[t][:, :]
                    mm(o, hid_hi[f % 2][:, s], feed.w2(0, f), start=f == 0, stop=False)
                    mm(o, hid_hi[f % 2][:, s], feed.w2(1, f), start=False, stop=False)
                    last = mm(o, hid_lo[f % 2][:, s], feed.w2(0, f), start=False, stop=f == FT - 1)
                    if f == FT - 1:
                        last.then_inc(f_out_ps, 1)
                        last = None
                if last is not None:
                    last.then_inc(f_hid_used, 1)

            def setup():
                pe_eng.wait_ge(f_const, 2)
                for c in range(DC):
                    transpose_rows(0, 0, 0, c)
                pe_eng.wait_ge(feed.hi_ready, feed.HALVES)
                pe_eng.wait_ge(feed.lo_ready, feed.HALVES)

            def do_pass(r, par, i, last=False):
                for f in range(FT):
                    hidden(r, f)
                    if f == FT - 1 and not last:
                        transpose_rows(r + 1, 1 - par, i + par, 0)
                        transpose_rows(r + 1, 1 - par, i + par, 1)
                    if f:
                        outcome(r, f - 1)
                if not last:
                    transpose_rows(r + 1, 1 - par, i + par, 2)
                    transpose_rows(r + 1, 1 - par, i + par, 3)
                outcome(r, FT - 1)

            schedule(setup, do_pass, pe_eng.Fori)

        @block.scalar
        def _(act):
            def rows_raw(r, c):
                act.wait_ge(f_t, r * DC + c + 1)
                if not (isinstance(r, int) and r == 0 and c < 2):
                    act.wait_ge(f_t_lo, r * DC + c - 1)
                act.activation(z_t[c % 2][:, :], t_ps[c % 2][:, :], ACT.Identity, bias=bias2_c[:, c:c + 1],
                               scale=gain2_c[:, c:c + 1]).then_inc(f_t_raw, 1)

            def setup():
                act.wait_ge(f_columns, 16 * 3)
                for c in range(DC):
                    rows_raw(0, c)

            def do_pass(r, par, i, last=False):
                for f in range(FT):
                    n = r * FT + f
                    act.wait_ge(f_hid_ps, n + 1)
                    if not (isinstance(r, int) and r == 0 and f < 2):
                        act.wait_ge(f_hid_lo, n - 1)
                    act.activation(hid[f % 2][:, :], hid_ps[f % 2][:, :], ACT.Gelu, bias=b1_c[:, f:f + 1])\
                        .then_inc(f_hid, 1)
                if not last:
                    for c in range(DC):
                        rows_raw(r + 1, c)

            schedule(setup, do_pass, act.Fori)

        @block.vector
        def _(dve):
            def rows_split(r, c):
                dve.wait_ge(f_t_raw, r * DC + c + 1)
                dve.tensor_copy(z_t_hi[:, c, :], z_t[c % 2][:, :]).then_inc(f_t_hi, 1)
                dve.wait_ge(f_t_hi, r * DC + c + 1)
                dve.tensor_tensor(z_t_lo[:, c, :], z_t[c % 2][:, :], z_t_hi[:, c, :].bitcast(F32), ALU.subtract)\
                    .then_inc(f_t_lo, 1)

            def setup():
                for c in range(DC):
                    rows_split(0, c)

            def split(r, f):
                n = r * FT + f
                dve.wait_ge(f_hid, n + 1)
                if not (isinstance(r, int) and r == 0 and f < 2):
                    if f >= 2:
                        dve.wait_ge(f_hid_used, r * (FT - 1) + f - 1)
                    elif f == 1:
                        dve.wait_ge(f_out_ps, r * RT)
                    else:
                        dve.wait_ge(f_hid_used, r * (FT - 1))
                dve.tensor_copy(hid_hi[f % 2][:, :], hid[f % 2][:, :]).then_inc(f_hid_hi, 1)
                dve.wait_ge(f_hid_hi, n + 1)
                dve.tensor_tensor(hid_lo[f % 2][:, :], hid[f % 2][:, :], hid_hi[f % 2][:, :].bitcast(F32), ALU.subtract)\
                    .then_inc(f_hid_lo, 1)

            def moments(r, par):
                for t in range(RT):
                    dve.wait_ge(f_sum, r * RT + t + 1)
                    dve.bn_stats(stats[:, t, :], z[par][:, t, :]).then_inc(f_stats, 1)

            def spread(r):
                for t in range(RT):
                    dve.wait_ge(f_stats, r * 2 * RT + t + 1)
                    hold(dve, f_passed["dve"])
                    dve.bn_aggr(mv[:, t, :], stats[:, t, :]).then_inc(f_stats, 1)
                dve.wait_ge(f_stats, (r + 1) * 2 * RT)
                dve.tensor_scalar(var[:, :], mv[:, :, 1], LN_EPS, None, ALU.add).then_inc(f_var, 1)

            def normalise(r, par):
                dve.wait_ge(f_rstd, r + 1)
                for t in range(RT):
                    dve.tensor_scalar(z[par][:, t, :], z[par][:, t, :], mv[:, t, 0:1], rstd[:, t:t + 1],
                                      ALU.subtract, ALU.mult).then_inc(f_norm, 1)

            def sums(r, par):
                for t in range(RT):
                    dve.wait_ge(f_out_ps, r * RT + t + 1)
                    dve.wait_ge(f_node, r * RT + t + 1)
                    dve.tensor_tensor(z[par][:, t, :], out_ps[t][:, :], z[par][:, t, :], ALU.add).then_inc(f_sum, 1)

            def do_pass(r, par, i, last=False):
                for f in range(FT):
                    split(r, f)
                    if not (isinstance(r, int) and r == 0):
                        if f == 1:
                            moments(r - 1, 1 - par)
                            spread(r - 1)
                        if f == 3:
                            normalise(r - 1, 1 - par)
                if not last:
                    for c in range(DC):
                        rows_split(r + 1, c)
                sums(r, par)
                if last:
                    moments(r, par)
                    spread(r)
                    normalise(r, par)

            schedule(setup, do_pass, dve.Fori)


def build(nc, x, adj, adj_t, w, columns, bv1_row, bv2_row, peeled_rows, node_rows, w1, w2, gain2_col,
          bias2_col, b1_col, row_vectors, out):
    with ExitStack() as ctx:
        feed = FeedWeights(nc, ctx, w1, w2)
        attention_part(nc, x, adj, adj_t, w, columns, bv1_row, bv2_row, peeled_rows, node_rows, feed)
        feed_forward_part(nc, x, node_rows, feed, gain2_col, bias2_col, b1_col, row_vectors, out)


def kernel(**inputs):
    import numpy as np
    import concourse.bacc as bacc
    from concourse.bass_utils import run_bass_kernel_spmd

    nc = bacc.Bacc("TRN2", target_bir_lowering=False, num_devices=1, dynamic_dma_scratch_size=1024)
    arrays = {}

    def given(name, a):
        a = np.ascontiguousarray(a)
        arrays[name] = a
        return nc.dram_tensor(name, a.shape, mybir.dt.from_np(a.dtype), kind="ExternalInput").ap()

    def vector(name):
        return np.asarray(inputs["L0_gnn_" + name])

    def column(name):
        return vector(name).reshape(-1, P).T

    def row(name):
        return given(name + "_row", vector(name).reshape(1, -1))

    x = given("x", np.asarray(inputs["x"]).reshape(B * N, D))
    a = np.asarray(inputs["adj"])
    adj = given("adj", a.reshape(B * N, N))
    adj_t = given("adj_t", a.transpose(0, 2, 1).reshape(B * N, N))
    w = {n: given(n, vector(n).T) for n in WEIGHTS}
    columns = {n: given(n + "_c", column(n)) for n in COLUMN_VECTORS}
    bv1, bv2 = row("n2e_v_b"), row("e2n_v_b")
    w1, w2 = given("ffn_w1", vector("ffn_w1").T), given("ffn_w2", vector("ffn_w2").T)
    gain2_c, bias2_c = given("gain2_in", column("norm2_g")), given("bias2_in", column("norm2_b"))
    b1_c = given("b1_in", column("ffn_b1"))
    row_vectors = [row(n) for n in ("norm2_g", "norm2_b", "norm3_g", "norm3_b", "ffn_b2")]
    pe_rows = nc.dram_tensor("pe_rows", [B * N, D], F32).ap()
    node_rows = nc.dram_tensor("node_rows", [B * N, D], F32).ap()
    out = nc.dram_tensor("out", [B * N, D], F32, kind="ExternalOutput").ap()
    build(nc, x, adj, adj_t, w, columns, bv1, bv2, pe_rows, node_rows, w1, w2, gain2_c, bias2_c, b1_c,
          row_vectors, out)
    r = run_bass_kernel_spmd(nc, [arrays], core_ids=[0])
    return r.results[0]["out"].reshape(B, N, D)
```
